# Optimizing a Trainium2 kernel written in Bass

```python
import numpy as np
import jax
import jax.numpy as jnp

def _softmax(x, axis=-1):
    return jax.nn.softmax(x, axis=axis)

def _gelu(x):
    return jax.nn.gelu(x, approximate=True)

def _silu(x):
    return jax.nn.silu(x)

def _sigmoid(x):
    return jax.nn.sigmoid(x)

def _layernorm(x, axis=-1, eps=1e-05):
    m = jnp.mean(x, axis=axis, keepdims=True)
    v = jnp.var(x, axis=axis, keepdims=True)
    return (x - m) / jnp.sqrt(v + eps)

def _scatter_add(tgt, idx, src, axis=0):
    return tgt.at[idx].add(src)

def _segment_sum(src, seg, n):
    return jax.ops.segment_sum(src, seg, n)
kernel_name = 'mk_adj_resnorm_d4_adj_r2_d7a6da'

def setup_inputs(seed: int=0):
    np.random.seed(seed)
    _w = jnp.asarray

    def _rec_inputs():
        import jax
        import jax.numpy as jnp
        _gk = jax.random.key(seed)
        x = -0.0005207 + 1.001 * jax.random.normal(jax.random.fold_in(_gk, 1), (128, 64, 256), jnp.float32)
        _a = jax.random.bernoulli(jax.random.fold_in(_gk, 2), 0.125, (128, 64, 64))
        _af = _a.astype(jnp.float32)
        adj = _af
        _nm = jnp.ones((128, 64), dtype=bool)
        nodemask = _nm
        return (x, adj, nodemask)
    x, adj, nodemask = _rec_inputs()

    def _L0_gnn_setup():
        import jax, jax.numpy as jnp
        import numpy as np
        HEADS = 8
        DIM_HEAD = 64
        LA = 0.33
        LD = 0.33
        LG = 0.33
        key = jax.random.key(seed)
        ks = jax.random.split(key, 6)
        B, N, D = (4, 512, 256)
        inner = HEADS * DIM_HEAD
        x = jax.random.normal(ks[0], (B, N, D), jnp.float32)
        mask = jax.random.uniform(ks[1], (B, N)) < 0.9
        adjacency_mat = (jax.random.uniform(ks[2], (B, N, N)) < 0.05).astype(jnp.float32)
        distance_mat = jax.random.uniform(ks[3], (B, N, N), jnp.float32) * 5.0
        W_qkv = jax.random.normal(ks[4], (D, inner * 3), jnp.float32) * 0.02
        W_out = jax.random.normal(ks[5], (inner, D), jnp.float32) * 0.02
        b_out = jnp.zeros((D,), jnp.float32)
        return {'x': x, 'mask': mask, 'adjacency_mat': adjacency_mat, 'distance_mat': distance_mat, 'W_qkv': W_qkv, 'W_out': W_out, 'b_out': b_out}
    _L0_gnn_all = _L0_gnn_setup()
    _L0_gnn_in = {k: v for k, v in _L0_gnn_all.items() if k in ('W_qkv', 'W_out', 'b_out')}
    del _L0_gnn_all

    def _L1_gnn_setup():
        import jax, jax.numpy as jnp
        import numpy as np
        EPS = 1e-06
        key = jax.random.key(seed)
        k1, k2, k3 = jax.random.split(key, 3)
        B, N, F, O = (8, 2048, 256, 256)
        x = jax.random.normal(k1, (B, N, F), dtype=jnp.float32)
        adj = jax.random.uniform(k2, (B, N, N), dtype=jnp.float32)
        W = jax.random.normal(k3, (O, 2 * F), dtype=jnp.float32) * (1.0 / np.sqrt(2 * F))
        return {'x': x, 'adj': adj, 'W': W}
    _L1_gnn_all = _L1_gnn_setup()
    _L1_gnn_in = {k: v for k, v in _L1_gnn_all.items() if k in ('W',)}
    del _L1_gnn_all

    def _L2_gnn_setup():
        import jax, jax.numpy as jnp
        import numpy as np
        EPS_LN = 1e-05

        def hypergraph_conv(x, adj, W, b):
            N, C, _ = adj.shape
            H = (adj != 0).astype(x.dtype)
            w = adj.reshape(N, -1)[:, :C]
            xw = jnp.einsum('ncd,hd->nch', x, W)
            Dn = jnp.einsum('nce,ne->nc', H, w)
            Dn = jnp.where(Dn > 0, 1.0 / Dn, 0.0)
            Be = H.sum(axis=1)
            Be = jnp.where(Be > 0, 1.0 / Be, 0.0)
            m = Be[:, :, None] * jnp.einsum('nce,nch->neh', H, xw)
            out = Dn[:, :, None] * jnp.einsum('nce,neh->nch', H, m)
            return out + b

        def layer_norm(x, g, b):
            mu = jnp.mean(x, axis=-1, keepdims=True)
            var = jnp.var(x, axis=-1, keepdims=True)
            return (x - mu) * jax.lax.rsqrt(var + EPS_LN) * g + b
        key = jax.random.key(seed)
        ks = jax.random.split(key, 4)
        N, C, Din, Dh, Dout = (16, 512, 256, 512, 256)
        x = jax.random.normal(ks[0], (N, C, Din), dtype=jnp.float32)
        adj = jax.random.uniform(ks[1], (N, C, C), dtype=jnp.float32, minval=0.1, maxval=1.0)
        W1 = jax.random.normal(ks[2], (Dh, Din), dtype=jnp.float32) * (1.0 / np.sqrt(Din))
        b1 = jnp.zeros((Dh,), dtype=jnp.float32)
        gamma = jnp.ones((Dh,), dtype=jnp.float32)
        beta = jnp.zeros((Dh,), dtype=jnp.float32)
        W2 = jax.random.normal(ks[3], (Dout, Dh), dtype=jnp.float32) * (1.0 / np.sqrt(Dh))
        b2 = jnp.zeros((Dout,), dtype=jnp.float32)
        return {'x': x, 'adj': adj, 'W1': W1, 'b1': b1, 'gamma': gamma, 'beta': beta, 'W2': W2, 'b2': b2}
    _L2_gnn_all = _L2_gnn_setup()
    _L2_gnn_in = {k: v for k, v in _L2_gnn_all.items() if k in ('W1', 'b1', 'gamma', 'beta', 'W2', 'b2')}
    del _L2_gnn_all

    def _L3_gnn_setup():
        import math
        import jax, jax.numpy as jnp
        import numpy as np
        B, N, D = (8, 1024, 256)
        key = jax.random.key(seed)
        ks = jax.random.split(key, 9)
        s = 1.0 / math.sqrt(D)
        return {'x': jax.random.normal(ks[0], (B, N, D), dtype=jnp.float32), 'adj': jax.random.uniform(ks[1], (B, N, N), dtype=jnp.float32), 'Wqk': jax.random.normal(ks[2], (D, D), dtype=jnp.float32) * s, 'bqk': jax.random.normal(ks[3], (D,), dtype=jnp.float32) * s, 'Wl': jax.random.normal(ks[4], (D, D), dtype=jnp.float32) * s, 'bl': jax.random.normal(ks[5], (D,), dtype=jnp.float32) * s, 'Wr': jax.random.normal(ks[6], (D, D), dtype=jnp.float32) * s, 'Wd': jax.random.normal(ks[7], (D, 1), dtype=jnp.float32), 'bd': jax.random.normal(ks[8], (D,), dtype=jnp.float32)}
    _L3_gnn_all = _L3_gnn_setup()
    _L3_gnn_in = {k: v for k, v in _L3_gnn_all.items() if k in ('Wqk', 'bqk', 'Wl', 'bl', 'Wr', 'Wd', 'bd')}
    del _L3_gnn_all
    return {'x': x, 'adj': adj, 'nodemask': nodemask, 'L0_gnn_W_qkv': _L0_gnn_in['W_qkv'], 'L0_gnn_W_out': _L0_gnn_in['W_out'], 'L0_gnn_b_out': _L0_gnn_in['b_out'], 'L1_gnn_W': _L1_gnn_in['W'], 'L2_gnn_W1': _L2_gnn_in['W1'], 'L2_gnn_b1': _L2_gnn_in['b1'], 'L2_gnn_gamma': _L2_gnn_in['gamma'], 'L2_gnn_beta': _L2_gnn_in['beta'], 'L2_gnn_W2': _L2_gnn_in['W2'], 'L2_gnn_b2': _L2_gnn_in['b2'], 'L3_gnn_Wqk': _L3_gnn_in['Wqk'], 'L3_gnn_bqk': _L3_gnn_in['bqk'], 'L3_gnn_Wl': _L3_gnn_in['Wl'], 'L3_gnn_bl': _L3_gnn_in['bl'], 'L3_gnn_Wr': _L3_gnn_in['Wr'], 'L3_gnn_Wd': _L3_gnn_in['Wd'], 'L3_gnn_bd': _L3_gnn_in['bd']}

def reference(x, adj, nodemask, L0_gnn_W_qkv, L0_gnn_W_out, L0_gnn_b_out, L1_gnn_W, L2_gnn_W1, L2_gnn_b1, L2_gnn_gamma, L2_gnn_beta, L2_gnn_W2, L2_gnn_b2, L3_gnn_Wqk, L3_gnn_bqk, L3_gnn_Wl, L3_gnn_bl, L3_gnn_Wr, L3_gnn_Wd, L3_gnn_bd):
    import jax
    import jax.numpy as jnp

    def _L0_gnn_ref(x, mask, adjacency_mat, distance_mat, W_qkv, W_out, b_out):
        import jax, jax.numpy as jnp
        import numpy as np
        HEADS = 8
        DIM_HEAD = 64
        LA = 0.33
        LD = 0.33
        LG = 0.33
        B, N, _ = x.shape
        scale = DIM_HEAD ** (-0.5)
        qkv = (x @ W_qkv).reshape(B, N, HEADS, 3, DIM_HEAD)
        q, k, v = (jnp.transpose(qkv[..., i, :], (0, 2, 1, 3)) for i in range(3))
        dots = jnp.einsum('bhid,bhjd->bhij', q, k) * scale
        big = jnp.finfo(dots.dtype).max
        m2 = mask[:, None, :, None] & mask[:, None, None, :]
        dots = jnp.where(m2, dots, -big)
        attn = jax.nn.softmax(dots, axis=-1) * LA
        adj = jnp.where(m2, adjacency_mat[:, None], 0.0)
        dist = jnp.where(m2, distance_mat[:, None], big)
        attn = attn + LG * adj + LD * jnp.exp(-dist)
        out = jnp.einsum('bhij,bhjd->bhid', attn, v)
        out = jnp.transpose(out, (0, 2, 1, 3)).reshape(B, N, HEADS * DIM_HEAD)
        return out @ W_out + b_out

    def _L1_gnn_ref(x, adj, W):
        import jax, jax.numpy as jnp
        import numpy as np
        EPS = 1e-06
        deg = jnp.sum(adj, axis=-1, keepdims=True)
        agg = jnp.einsum('bij,bjf->bif', adj, x) / jnp.maximum(deg, EPS)
        cat = jnp.concatenate([x, agg], axis=2)
        out = jnp.einsum('bnf,of->bno', cat, W)
        return jax.nn.relu(out)

    def _L2_gnn_ref(x, adj, W1, b1, gamma, beta, W2, b2):
        import jax, jax.numpy as jnp
        import numpy as np
        EPS_LN = 1e-05

        def hypergraph_conv(x, adj, W, b):
            N, C, _ = adj.shape
            H = (adj != 0).astype(x.dtype)
            w = adj.reshape(N, -1)[:, :C]
            xw = jnp.einsum('ncd,hd->nch', x, W)
            Dn = jnp.einsum('nce,ne->nc', H, w)
            Dn = jnp.where(Dn > 0, 1.0 / Dn, 0.0)
            Be = H.sum(axis=1)
            Be = jnp.where(Be > 0, 1.0 / Be, 0.0)
            m = Be[:, :, None] * jnp.einsum('nce,nch->neh', H, xw)
            out = Dn[:, :, None] * jnp.einsum('nce,neh->nch', H, m)
            return out + b

        def layer_norm(x, g, b):
            mu = jnp.mean(x, axis=-1, keepdims=True)
            var = jnp.var(x, axis=-1, keepdims=True)
            return (x - mu) * jax.lax.rsqrt(var + EPS_LN) * g + b
        h = jax.nn.relu(hypergraph_conv(x, adj, W1, b1))
        h = layer_norm(h, gamma, beta)
        y = hypergraph_conv(h, adj, W2, b2)
        return y + x

    def _L3_gnn_ref(x, adj, Wqk, bqk, Wl, bl, Wr, Wd, bd):
        import math
        import jax, jax.numpy as jnp
        import numpy as np
        B, N, D = (8, 1024, 256)
        deg = jnp.sum(adj, axis=-1, keepdims=True)
        gate = jax.nn.sigmoid(deg * Wd[:, 0] + bd)
        xg = x * gate
        QK = jax.nn.sigmoid(xg @ Wqk.T + bqk)
        scores = jnp.einsum('bnd,bmd->bnm', QK, QK) / math.sqrt(D)
        scores = scores * adj
        attn = scores / (jnp.sum(scores, axis=-1, keepdims=True) + 1e-06)
        out = jnp.einsum('bnm,bmd->bnd', attn, xg)
        out = out @ Wl.T + bl + xg @ Wr.T
        return jax.nn.relu(out)
    x = _layernorm(x + _L0_gnn_ref(x, nodemask, adj, adj, L0_gnn_W_qkv, L0_gnn_W_out, L0_gnn_b_out), axis=-1)
    x = _layernorm(x + _L1_gnn_ref(x, adj, L1_gnn_W), axis=-1)
    x = _layernorm(x + _L2_gnn_ref(x, adj, L2_gnn_W1, L2_gnn_b1, L2_gnn_gamma, L2_gnn_beta, L2_gnn_W2, L2_gnn_b2), axis=-1)
    x = _layernorm(x + _L3_gnn_ref(x, adj, L3_gnn_Wqk, L3_gnn_bqk, L3_gnn_Wl, L3_gnn_bl, L3_gnn_Wr, L3_gnn_Wd, L3_gnn_bd), axis=-1)
    return x

_drawn_inputs = setup_inputs


def setup_inputs(seed=0):
    import zlib

    import numpy as np

    out = dict(_drawn_inputs(seed))
    spreads = {'L0_gnn_b_out': (0.0, 0.1),
     'L2_gnn_b1': (0.0, 0.1),
     'L2_gnn_gamma': (1.0, 0.2),
     'L2_gnn_beta': (0.0, 0.1),
     'L2_gnn_b2': (0.0, 0.1)}
    factors = {}
    for name, (base, spread) in spreads.items():
        noise = np.random.default_rng([zlib.crc32(name.encode()), seed]).standard_normal(out[name].shape)
        drawn = base * np.exp(spread * noise) if base else spread * noise
        out[name] = jnp.asarray(drawn.astype(out[name].dtype))
    for name, factor in factors.items():
        out[name] = (out[name] * factor).astype(out[name].dtype)
    return out
```

```python
from contextlib import ExitStack

import concourse.bass as bass
from concourse import mybir

ALU = mybir.AluOpType
ACT = mybir.ActivationFunctionType
AX = mybir.AxisListType
F32 = mybir.dt.float32
BF16 = mybir.dt.bfloat16
U8 = mybir.dt.uint8

P = 128
N = 64
D = 256
B = 128
H = 8
DH = 64
HID = 512
T = 4
GRP = B * N // (T * P)
TOK = T * P
C = D // P
HP = H // 2
HC = HID // P
EPS_LN = 1e-5
MIX = 0.33
BIG = 2.0 ** 120

SCHEDULE = [
    ("A", "mixmat", 0), ("B", "turn1", 0), ("A", "q", 0), ("B", "graph_a", 0), ("B", "turn1", 1), ("A", "q", 1),
    ("B", "graph_b", 0), ("A", "q", 2), ("B", "graph_c", 0), ("A", "q", 3), ("B", "agg", 0), ("B", "agg", 1),
    ("B", "graph_d", 0),
    ("B", "mean", 0), ("B", "mean", 1), ("A", "k", 0), ("A", "k", 1), ("A", "k", 2),
    ("B", "spread", 0), ("B", "spread", 1), ("A", "k", 3),
    ("B", "up", 0), ("B", "up", 1), ("A", "v", 0), ("B", "up", 2), ("B", "up", 3), ("A", "v", 1), ("A", "v", 2),
    ("B", "turn_h", 0), ("B", "turn_h", 1), ("A", "v", 3), ("B", "turn_h", 2), ("B", "turn_h", 3),
    ("A", "score", 0), ("B", "down", 0), ("B", "down", 1),
    ("B", "hyper", 0), ("B", "hyper", 1), ("A", "score", 1), ("A", "head", 0),
    ("B", "turn3", 0), ("B", "turn3", 1), ("A", "head", 1), ("B", "qk", 0), ("B", "qk", 1),
    ("A", "head", 2), ("B", "sim", 0), ("A", "head", 3), ("B", "turn_s", 0), ("A", "out0", 0),
    ("B", "agg3", 0), ("B", "agg3", 1), ("A", "out0", 1), ("B", "out3", 0), ("B", "out3", 1),
]

FILLS = {"mixmat": ["mixmat"], "graph_a": ["ht"], "graph_b": ["cnt"], "graph_c": ["sym", "meanT"], "graph_d": ["gT"],
         "score": ["s_even", "s_odd"], "head": ["pT", "oT"]}
BANK = {}
PER_BANK = [0] * 8
for _s, _n, _i in SCHEDULE:
    for _f in FILLS.get(_n, [_n]):
        _k = sum(1 for (f, i), (b, c) in BANK.items() if (b < 4) == (_s == "A")) % 4 + (0 if _s == "A" else 4)
        BANK[(_f, _i)] = (_k, PER_BANK[_k])
        PER_BANK[_k] += 1

BEFORE = {}
for _key, (_b, _c) in BANK.items():
    _prev = (_c - 1) % PER_BANK[_b]
    BEFORE[_key] = (_b, next(k for k, v in BANK.items() if v == (_b, _prev)), 1 if _c == 0 else 0)
READ_OUT = {
    "mixmat": "mm_ready", "q": "q_ready", "k": "k_ready", "v": "v_ready",
    "pT": "pT_ready", "oT": "oT_ready", "out0": "sum0_ready",
    "turn1": "turn1_ready", "agg": "agg_ready", "mean": "sum1_ready", "ht": "ht_ready", "cnt": "dsafe",
    "sym": "g_ready", "meanT": "meanT_ready", "gT": "gT_ready", "spread": "spread_ready",
    "up": "relu_ready", "down": "down_ready", "hyper": "sum2_ready", "turn3": "turn3_ready",
    "qk": "qk_tanh", "sim": "sim_ready", "turn_s": "sT_ready", "agg3": "agg3_ready", "out3": "sum3_ready",
}

PER = {
    "xT_in": 32, "x_in": 16, "adjA_in": 16, "adjB_in": 32, "adjC_in": 32, "out_done": 32,
    "xb_ready": 1, "expA_ready": 1, "mm_ready": 1, "mix_sum": 1, "mix_ready": 1,
    "q_ready": 4, "k_ready": 4, "v_ready": 4,
    "max_ready": 4, "shift_ready": 4, "exp_ready": 4, "sum_ready": 4, "rsum_ready": 8, "prob_ready": 4,
    "attn_ready": 4, "pT_ready": 4, "oT_ready": 4,
    "sum0_ready": 2, "stats0": 4, "mv0": 4, "var0": 2, "rstd0": 2, "x1_ready": 2,
    "turn1_ready": 2, "agg_ready": 2,
    "edge_ready": 1, "deg_ready": 1, "degmax": 1, "rdeg_ready": 1, "meanA_ready": 1, "ht_ready": 1,
    "cntmax": 1, "be_ready": 1, "bht_ready": 1, "dsign": 2, "dsafe": 1, "drec": 1, "dn_ready": 1,
    "g_ready": 1, "meanT_ready": 1, "gT_ready": 1,
    "sum1_ready": 2, "stats1": 4, "mv1": 4, "var1": 2, "rstd1": 2, "x2_ready": 2,
    "spread_ready": 2, "relu_ready": 4, "stats_h": 4, "mv_h": 4, "var_h": 4, "rstd_h": 4, "h_ready": 4,
    "hT_act": 2, "hT_dve": 2, "down_ready": 2,
    "sum2_ready": 2, "stats2": 4, "mv2": 4, "var2": 2, "rstd2": 2, "x3_ready": 2,
    "z_ready": 4, "gate_ready": 2, "xg_ready": 2, "turn3_ready": 2, "qk_tanh": 2, "qk_ready": 2,
    "sim_ready": 1, "simsum": 1, "simeps": 1, "simrec": 1, "s_ready": 1, "sT_ready": 1, "agg3_ready": 2,
    "sum3_ready": 2, "stats3": 4, "mv3": 4, "var3": 2, "rstd3": 2, "x4_ready": 2,
}


def graph_layers(nc, x, x_t, adj, adj_row0, mask_u8, wqkv, w_out, b_out, w_mean_t, w1_t, b1, gamma_c, beta_c, w2_t, b2,
                 wqk_t, bqk_c, wl_t, bl, wr_t, wd_r, bd_r, ident_c, ones3_c, mrow_c, out):
    with ExitStack() as ctx:
        def sb(name, shape, dt=F32):
            return ctx.enter_context(nc.sbuf_tensor(name, shape, dt))

        wq = sb("wq", [P, C, H * DH])
        wk = sb("wk", [P, C, H * DH])
        wv = sb("wv", [P, C, H * DH])
        wo = sb("wo", [P, HP, D])
        wm = sb("wm", [P, 2 * C, D])
        w1 = sb("w1", [P, C, HID])
        w2 = sb("w2", [P, HC, D])
        wqk = sb("wqk", [P, C, D])
        wlr = sb("wlr", [P, 2 * C, D])
        ident = sb("ident", [P, P])
        identb = sb("identb", [P, P], BF16)
        onesf = sb("onesf", [P, P])
        ones3 = sb("ones3", [P, P], BF16)
        onescol = sb("onescol", [P, 2], BF16)
        biasrow = sb("biasrow", [1, HID + 2 * D])
        biasrem = sb("biasrem", [1, 2, HID + 2 * D])
        bias3 = sb("bias3", [96, HID + 2 * D], BF16)
        bout = sb("bout", [P, D])
        wd = sb("wd", [P, D])
        bd = sb("bd", [P, D])
        gam = sb("gam", [P, HC])
        bet = sb("bet", [P, HC])
        bqk = sb("bqk", [P, C])
        row0 = sb("row0", [P, T * GRP])
        negh = sb("negh", [P, T])
        mcst = sb("mcst", [4, 1 + P])
        mi = sb("mi", [4, T * GRP, P], BF16)
        mj = sb("mj", [4, T * GRP, N], BF16)
        xT = sb("xT", [P, C, TOK])
        xin = sb("xin", [P, T, D])
        adjA = sb("adjA", [P, T, N])
        expA = sb("expA", [P, T, N])
        mm01 = sb("mm01", [P, T, N])
        mix = sb("mix", [P, T, N])
        qT = sb("qT", [P, HP, TOK])
        kT = sb("kT", [P, HP, TOK])
        v = sb("v", [P, T, 2, HP, DH])
        prob = sb("prob", [P, T, HP, 2, N])
        smax = sb("smax", [P, T, 2 * HP])
        ssum = sb("ssum", [P, T, 2 * HP])
        ssc = sb("ssc", [P, T, 2 * HP])
        srec = sb("srec", [P, T, 2 * HP])
        pT = sb("pT", [P, 2, HP, P])
        oT = qT
        adjB = sb("adjB", [P, T, P])
        adjC = sb("adjC", [P, T, P])
        edge = sb("edge", [P, T, P], BF16)
        deg = sb("deg", [P, T])
        degm = sb("degm", [P, T])
        rdeg = sb("rdeg", [P, T])
        meanA = sb("meanA", [P, T, P])
        meanT = sb("meanT", [P, T, P])
        hT0 = sb("hT0", [P, T, P])
        bhT = sb("bhT", [P, T, P])
        cntm = sb("cntm", [P, T])
        be = sb("be", [P, T])
        dpos = sb("dpos", [P, T])
        dneg = sb("dneg", [P, T])
        dsafe = sb("dsafe", [P, T])
        drec = sb("drec", [P, T])
        dn = sb("dn", [P, T])
        gmat = sb("gmat", [P, T, P])
        gT = sb("gT", [P, T, P])
        x1T = sb("x1T", [P, C, TOK])
        aggT = sb("aggT", [P, C, TOK])
        spT = sb("spT", [P, C, TOK])
        r = sb("r", [P, T, HID])
        hT = sb("hT", [P, HC, TOK])
        yw = sb("yw", [P, T, D])
        gate = sb("gate", [P, T, D])
        xg = gate
        xgT, qkT, agg3 = x1T, aggT, spT
        sim = sb("sim", [P, T, P])
        simsum = sb("simsum", [P, T])
        simeps = sb("simeps", [P, T])
        simrec = sb("simrec", [P, T])
        smat = sim
        sT = sb("sT", [P, T, P])
        pre = [sb(f"pre{i}", [P, T, D]) for i in range(2)]
        xl = [sb(f"x{i + 1}", [P, T, D]) for i in range(3)]
        xl.append(xl[1])
        mi_u8 = r[0:4, :, :].rearrange("p t n -> p (t n)").bitcast(U8).rearrange("p (t n) -> p t n", n=P)
        mj_u8 = hT[0:4, 0:2, :].rearrange("p t n -> p (t n)").bitcast(U8).rearrange("p (t n) -> p t n", n=N)
        stats = [sb(f"stats{i}", [P, T, 6]) for i in range(5)]
        mv = [sb(f"mv{i}", [P, T, 2]) for i in range(5)]
        var = [sb(f"var{i}", [P, T]) for i in range(5)]
        rstd = [sb(f"rstd{i}", [P, T]) for i in range(5)]

        bank = [ctx.enter_context(nc.psum_tensor(f"bank{i}", [P, 512], F32)) for i in range(8)]
        SEM = {n: ctx.enter_context(nc.semaphore(n)) for n in PER}
        full = [ctx.enter_context(nc.semaphore(f"bank{i}_full")) for i in range(8)]
        weights_in = ctx.enter_context(nc.semaphore("weights_in"))
        early_in = ctx.enter_context(nc.semaphore("early_in"))
        zero_ready = ctx.enter_context(nc.semaphore("zero_ready"))
        parted = ctx.enter_context(nc.semaphore("parted"))
        setup_dve = ctx.enter_context(nc.semaphore("setup_dve"))

        def count(sem, g, k, back=0):
            n = g * PER[sem] + (k - back * PER[sem])
            return (zero_ready, 4) if isinstance(n, int) and n <= 0 else (SEM[sem], n)

        def apart(eng, g):
            if not isinstance(g, int):
                eng.sem_inc(parted, 1)

        def unit(k):
            return prob[:, k - k % 2:k - k % 2 + 2, :, k % 2, :]

        def rows_of(ap):
            return ap.rearrange("p t h n -> p (t h) n")

        def bank_of(fill, i):
            return bank[BANK[(fill, i)][0]]

        def filled(fill, i, g, back=0):
            b, c = BANK[(fill, i)]
            n = g * PER_BANK[b] + (c + 1 - back * PER_BANK[b])
            return (zero_ready, 4) if isinstance(n, int) and n <= 0 else (full[b], n)

        def emptied(fill, i, g):
            b, (f, j), back = BEFORE[(fill, i)]
            if f == "turn_h":
                return count("hT_act" if j < 2 else "hT_dve", g, j % 2 + 1, back)
            if f in ("s_even", "s_odd"):
                return count("shift_ready", g, 2 * j + 1 + (f == "s_odd"), back)
            return count(READ_OUT[f], g, j + 1, back)

        def now_full(ins, fill, i):
            ins.then_inc(full[BANK[(fill, i)][0]], 1)

        def rounds(eng, body):
            body(0, None)
            body(1, 0)
            with eng.Fori(1, GRP - 1) as g:
                body(g + 1, g)
            body(None, GRP - 1)

        def run(steps, a, b):
            for stream, name, i in SCHEDULE:
                g = a if stream == "A" else b
                if g is not None and name in steps:
                    steps[name](g, i)

        x_g = x.rearrange("(g t h) n d -> g (h n) t d", t=T, h=2)
        out_g = out.rearrange("(g t h) n d -> g (h n) t d", t=T, h=2)
        xT_g = x_t.rearrange("(c p) (g n) -> g p c n", p=P, n=TOK)
        adj_g = adj.rearrange("(g t h) n m -> g (h n) t m", t=T, h=2)
        adj_h = adj.rearrange("(g t h) n m -> g h n t m", t=T, h=2)
        N_EARLY = 7
        N_WEIGHTS = 17

        block = ctx.enter_context(nc.Block())

        @block.sync
        def _(sp):
            sp.dma_start(mi_u8, mask_u8.rearrange("(t h) n -> (t h n)", h=2)
                         .rearrange("(a n) -> a n", a=1).broadcast_to([4, B * N])
                         .rearrange("a (t n) -> a t n", n=P)).then_inc(early_in, 16)
            for h in range(2):
                sp.dma_start(mj_u8[2 * h:2 * h + 2], mask_u8.rearrange("(a t h) n -> a h t n", a=1, h=2)[:, h]
                             .broadcast_to([2, T * GRP, N])).then_inc(early_in, 16)
            sp.dma_start(mcst[:, :], mrow_c).then_inc(early_in, 16)
            sp.dma_start(ident[:, :], ident_c).then_inc(early_in, 16)
            sp.dma_start(onesf[:, :], ones3_c).then_inc(early_in, 16)
            sp.dma_start(row0[:, :], adj_row0).then_inc(early_in, 16)
            wqkv_v = wqkv.rearrange("(c k) (h i d) -> i c k h d", k=P, h=H, i=3)

            def load(a, b):
                if a is not None:
                    sp.wait_ge(*count("mix_sum", a, 1, 1))
                    sp.dma_start(adjA[:, :, :], adj_g[a]).then_inc(SEM["adjA_in"], 16)
                if b is not None:
                    sp.wait_ge(*count("edge_ready", b, 1, 1))
                    sp.wait_ge(*count("deg_ready", b, 1, 1))
                    sp.wait_ge(*count("meanA_ready", b, 1, 1))
                    for h in range(2):
                        if isinstance(b, int) and b == 0:
                            sp.wait_ge(zero_ready, 1)
                        sp.dma_start(adjB[h * N:(h + 1) * N, :, h * N:(h + 1) * N],
                                     adj_h[b, h]).then_inc(SEM["adjB_in"], 16)
                if a is not None:
                    sp.wait_ge(*count("sum0_ready", a, 2, 1))
                    sp.dma_start(xin[:, :, :], x_g[a]).then_inc(SEM["x_in"], 16)
                    sp.wait_ge(*filled("v", T - 1, a, 1))
                    for c in range(C):
                        sp.dma_start(xT[:, c, :], xT_g[a][:, c, :]).then_inc(SEM["xT_in"], 16)
                if b is not None:
                    sp.wait_ge(*count("sim_ready", b, 1, 1))
                    for h in range(2):
                        if isinstance(b, int) and b == 0:
                            sp.wait_ge(zero_ready, 2)
                        sp.dma_start(adjC[h * N:(h + 1) * N, :, h * N:(h + 1) * N],
                                     adj_h[b, h]).then_inc(SEM["adjC_in"], 16)

            def store(b):
                for i in range(2):
                    sp.wait_ge(*count("x4_ready", b, i + 1))
                    sp.dma_start(out_g[b][:, 2 * i:2 * i + 2, :], xl[3][:, 2 * i:2 * i + 2, :]).then_inc(SEM["out_done"], 16)

            load(0, None)
            for i, w in enumerate((wq, wk, wv)):
                for c in range(C):
                    sp.dma_start(w[:, c, :].rearrange("p (h d) -> p h d", h=H), wqkv_v[i, c]).then_inc(weights_in, 16)
            for dst, src in ((wo, w_out), (wm, w_mean_t), (w1, w1_t), (w2, w2_t), (wqk, wqk_t)):
                sp.dma_start(dst[:, :, :], src.rearrange("(c k) n -> k c n", k=P)).then_inc(weights_in, 16)
            sp.dma_start(wlr[:, 0:C, :], wl_t.rearrange("(c k) n -> k c n", k=P)).then_inc(weights_in, 16)
            sp.dma_start(wlr[:, C:2 * C, :], wr_t.rearrange("(c k) n -> k c n", k=P)).then_inc(weights_in, 16)
            sp.dma_start(gam[:, :], gamma_c).then_inc(weights_in, 16)
            sp.dma_start(bet[:, :], beta_c).then_inc(weights_in, 16)
            sp.dma_start(bqk[:, :], bqk_c).then_inc(weights_in, 16)
            sp.dma_start(biasrow[:, 0:HID], b1.rearrange("(a n) -> a n", a=1)).then_inc(weights_in, 16)
            load(1, 0)
            with sp.Fori(1, GRP - 1) as g:
                load(g + 1, g)
                store(g - 1)
            load(None, GRP - 1)
            store(GRP - 2)
            store(GRP - 1)
            sp.wait_ge(*count("out_done", GRP - 1, 32))

        @block.gpsimd
        def _(pool):
            pool.memset(adjB[:, :, :], 0.0).then_inc(zero_ready, 1)
            pool.memset(adjC[:, :, :], 0.0).then_inc(zero_ready, 1)
            pool.memset(negh[:, :], -0.5)
            pool.memset(bias3[:, :], 0.0).then_inc(zero_ready, 1)
            pool.memset(onescol[:, :], 1.0).then_inc(zero_ready, 1)
            pool.wait_ge(zero_ready, 4)
            pool.wait_ge(weights_in, 16 * (N_WEIGHTS + 5))

            def mixmat(g, i):
                pool.wait_ge(*count("x_in", g, 16))
                pool.tensor_tensor(xin[:, :, :], xin[:, :, :],
                                   bout[:, :].rearrange("p (a d) -> p a d", a=1).broadcast_to([P, T, D]),
                                   ALU.add).then_inc(SEM["xb_ready"], 1)

            def inv_root(g, layer, name, lo, hi, k):
                pool.wait_ge(*count(f"mv{name}", g, hi))
                n = "_h" if layer == 4 else str(layer)
                apart(pool, g)
                pool.tensor_scalar(var[layer][:, lo:hi], mv[layer][:, lo:hi, 1], EPS_LN, None,
                                   ALU.add).then_inc(SEM[f"var{n}"], 1)
                pool.wait_ge(*count(f"var{n}", g, k + 1))
                pool.tensor_tensor(rstd[layer][:, lo:hi], var[layer][:, lo:hi], negh[:, lo:hi],
                                   ALU.pow).then_inc(SEM[f"rstd{n}"], 1)

            def graph_a(g, i):
                pool.wait_ge(*count("rdeg_ready", g, 1))
                pool.wait_ge(*count("adjB_in", g, 32))
                pool.wait_ge(*filled("meanT", 0, g, 1))
                pool.tensor_tensor(meanA[:, :, :], adjB[:, :, :],
                                   rdeg[:, :].rearrange("p (t a) -> p t a", a=1).broadcast_to([P, T, P]),
                                   ALU.mult).then_inc(SEM["meanA_ready"], 1)

            def graph_b(g, i):
                pool.wait_ge(*count("be_ready", g, 1))
                pool.wait_ge(*count("ht_ready", g, 1))
                pool.tensor_tensor(bhT[:, :, :], hT0[:, :, :],
                                   be[:, :].rearrange("p (t a) -> p t a", a=1).broadcast_to([P, T, P]),
                                   ALU.mult).then_inc(SEM["bht_ready"], 1)

            def qk(g, i):
                pool.wait_ge(*count("qk_tanh", g, i + 1))
                apart(pool, g)
                pool.tensor_scalar(qkT[:, i, :], qkT[:, i, :], 1.0, None, ALU.add).then_inc(SEM["qk_ready"], 1)

            steps = {
                "mixmat": mixmat, "graph_a": graph_a, "graph_b": graph_b, "qk": qk,
                "out0": lambda g, i: inv_root(g, 0, "0", 2 * i, 2 * i + 2, i),
                "mean": lambda g, i: inv_root(g, 1, "1", 2 * i, 2 * i + 2, i),
                "hyper": lambda g, i: inv_root(g, 2, "2", 2 * i, 2 * i + 2, i),
                "out3": lambda g, i: inv_root(g, 3, "3", 2 * i, 2 * i + 2, i),
                "up": lambda g, i: inv_root(g, 4, "_h", i, i + 1, i),
            }
            rounds(pool, lambda a, b: run(steps, a, b))

        @block.scalar
        def _(act):
            def row(ap, n=P):
                return ap.rearrange("(a n) -> a n", a=1).broadcast_to([n, ap.shape[0]])

            act.dma_start(biasrow[:, HID:HID + D], row(b2, 1)).then_inc(weights_in, 16)
            act.dma_start(biasrow[:, HID + D:HID + 2 * D], row(bl, 1)).then_inc(weights_in, 16)
            act.dma_start(bout[:, :], row(b_out)).then_inc(weights_in, 16)
            act.dma_start(wd[:, :], row(wd_r)).then_inc(weights_in, 16)
            act.dma_start(bd[:, :], row(bd_r)).then_inc(weights_in, 16)

            def copy_out(g, fill, i, dst, ready, func=ACT.Copy, **kw):
                act.wait_ge(*filled(fill, i, g))
                src = bank_of(fill, i)
                act.activation(dst, src[:, :], func, **kw).then_inc(SEM[ready], 1)

            def mixmat(g, i):
                act.wait_ge(*count("adjA_in", g, 16))
                act.activation(expA[:, :, :], adjA[:, :, :], ACT.Exp, scale=-1.0).then_inc(SEM["expA_ready"], 1)

            def val(g, i):
                act.wait_ge(*filled("v", i, g))
                src = bank_of("v", i)[:, :].rearrange("n (p e d) -> n e p d", e=2, d=DH)
                for gr in range(2):
                    for e in range(2):
                        ins = act.activation(v[e * N:(e + 1) * N, i, gr, :, :], src[gr * N:(gr + 1) * N, e], ACT.Copy)
                ins.then_inc(SEM["v_ready"], 1)

            def score(g, i):
                for k in range(2 * i, 2 * i + 2):
                    act.wait_ge(*count("shift_ready", g, k + 1))
                    act.activation(rows_of(unit(k)), rows_of(unit(k)), ACT.Exp,
                                   scale=float(DH) ** -0.5).then_inc(SEM["exp_ready"], 1)

            def head(g, i):
                copy_out(g, "pT", i, pT[:, i % 2].rearrange("p a n -> p (a n)"), "pT_ready")
                act.wait_ge(*filled("oT", i, g))
                src = bank_of("oT", i)
                ins = act.activation(oT[:, :, i * P:(i + 1) * P], src[:, :].rearrange("p (a n) -> p a n", a=HP), ACT.Copy)
                ins.then_inc(SEM["oT_ready"], 1)

            def flat(ap):
                return ap.rearrange("p t n -> p (t n)")

            def graph_a(g, i):
                act.wait_ge(*filled("ht", 0, g))
                src = bank_of("ht", 0)
                ins = act.activation(flat(hT0[:, :, :]), src[:, 0:T * P // 2].bitcast(BF16), ACT.Copy)
                ins.then_inc(SEM["ht_ready"], 1)

            def up(g, i):
                copy_out(g, "up", i, r[:, i, :], "relu_ready", ACT.Relu)

            def turn_h(g, i):
                if i < 2:
                    copy_out(g, "turn_h", i, hT[:, i, :], "hT_act", ACT.Identity, scale=gam[:, i:i + 1],
                             bias=bet[:, i:i + 1])

            def down(g, i):
                copy_out(g, "down", i, flat(yw[:, 2 * i:2 * i + 2, :]), "down_ready")

            def hyper(g, i):
                act.wait_ge(*count("z_ready", g, 2 * i + 2))
                act.activation(gate[:, 2 * i:2 * i + 2, :], gate[:, 2 * i:2 * i + 2, :], ACT.Tanh,
                               scale=0.5).then_inc(SEM["gate_ready"], 1)

            def qk(g, i):
                copy_out(g, "qk", i, qkT[:, i, :], "qk_tanh", ACT.Tanh, scale=0.25, bias=bqk[:, i:i + 1])

            steps = {
                "mixmat": mixmat, "v": val, "score": score, "head": head, "graph_a": graph_a, "up": up,
                "turn_h": turn_h, "down": down, "hyper": hyper, "qk": qk,
                "q": lambda g, i: copy_out(g, "q", i, qT[:, i, :], "q_ready"),
                "k": lambda g, i: copy_out(g, "k", i, kT[:, i, :], "k_ready"),
                "turn1": lambda g, i: copy_out(g, "turn1", i, x1T[:, i, :], "turn1_ready"),
                "agg": lambda g, i: copy_out(g, "agg", i, aggT[:, i, :], "agg_ready"),
                "graph_c": lambda g, i: copy_out(g, "meanT", 0, flat(meanT[:, :, :]), "meanT_ready"),
                "graph_d": lambda g, i: copy_out(g, "gT", 0, flat(gT[:, :, :]), "gT_ready"),
                "spread": lambda g, i: copy_out(g, "spread", i, spT[:, i, :], "spread_ready"),
                "turn3": lambda g, i: copy_out(g, "turn3", i, xgT[:, i, :], "turn3_ready"),
                "turn_s": lambda g, i: copy_out(g, "turn_s", 0, flat(sT[:, :, :]), "sT_ready"),
                "agg3": lambda g, i: copy_out(g, "agg3", i, agg3[:, i, :], "agg3_ready"),
            }
            rounds(act, lambda a, b: run(steps, a, b))

        @block.vector
        def _(dve):
            done = [0]

            def setup(ins):
                done[0] += 1
                ins.then_inc(setup_dve, 1)
                dve.wait_ge(setup_dve, done[0])

            dve.wait_ge(early_in, 16 * N_EARLY)
            setup(dve.scalar_tensor_tensor(out=mi[:, :, :], in0=mi_u8, scalar=mcst[:, 0:1],
                                           in1=mcst[:, 1:1 + P].rearrange("p (a n) -> p a n", a=1)
                                           .broadcast_to([4, T * GRP, P]), op0=ALU.max, op1=ALU.mult))
            setup(dve.tensor_scalar(mj[:, :, :], mj_u8, mcst[:, 0:1], None, ALU.max))
            setup(dve.tensor_copy(identb[:, :], ident[:, :]))
            setup(dve.tensor_copy(ones3[:, :], onesf[:, :]))
            dve.wait_ge(zero_ready, 4)
            dve.wait_ge(weights_in, 16 * (N_WEIGHTS + 5))
            setup(dve.tensor_copy(bias3[0:1, :], biasrow[:, :]))
            setup(dve.tensor_tensor(biasrem[:, 0, :], biasrow[:, :], bias3[0:1, :], ALU.subtract))
            setup(dve.tensor_copy(bias3[32:33, :], biasrem[:, 0, :]))
            setup(dve.tensor_copy(biasrem[:, 1, :], bias3[32:33, :]))
            setup(dve.tensor_tensor(biasrem[:, 1, :], biasrem[:, 0, :], biasrem[:, 1, :], ALU.subtract))
            setup(dve.tensor_copy(bias3[64:65, :], biasrem[:, 1, :]))
            setup(dve.tensor_scalar(wlr[:, :, :], wlr[:, :, :], 0.5, None, ALU.mult))
            setup(dve.tensor_scalar(bqk[:, :], bqk[:, :], 0.5, None, ALU.mult))

            def flat(ap):
                return ap.rearrange("p t n -> p (t n)")

            def wide(ap, n):
                return ap.rearrange("p (t a) -> p t a", a=1).broadcast_to([ap.shape[0], ap.shape[1], n])

            def norm(g, layer, name, src, dst, lo, hi, ready):
                n = "_h" if layer == 4 else str(layer)
                for t in range(lo, hi):
                    dve.bn_stats(stats[layer][:, t, :], src[:, t, :]).then_inc(SEM[f"stats{n}"], 1)
                for t in range(lo, hi):
                    dve.wait_ge(*count(f"stats{n}", g, t + 1))
                    apart(dve, g)
                    dve.bn_aggr(mv[layer][:, t, :], stats[layer][:, t, :]).then_inc(SEM[f"mv{n}"], 1)

            def scale(g, layer, src, dst, lo, hi, ready, k):
                n = "_h" if layer == 4 else str(layer)
                dve.wait_ge(*count(f"rstd{n}", g, k + 1))
                for t in range(lo, hi):
                    ins = dve.tensor_scalar(dst[:, t, :], src[:, t, :], mv[layer][:, t, 0:1],
                                            rstd[layer][:, t:t + 1], ALU.subtract, ALU.mult)
                ins.then_inc(SEM[ready], 1)

            def mixmat(g, i):
                dve.wait_ge(*filled("mixmat", 0, g))
                src = bank_of("mixmat", 0)
                ins = dve.tensor_scalar(flat(mm01[:, :, :]), src[:, 0:T * N], 1.0 / BIG, 1.0, ALU.mult, ALU.add)
                ins.then_inc(SEM["mm_ready"], 1)
                dve.wait_ge(*count("expA_ready", g, 1))
                dve.wait_ge(*count("adjA_in", g, 16))
                dve.tensor_tensor(mix[:, :, :], expA[:, :, :], adjA[:, :, :], ALU.add).then_inc(SEM["mix_sum"], 1)
                dve.wait_ge(*count("mm_ready", g, 1))
                dve.wait_ge(*count("mix_sum", g, 1))
                dve.scalar_tensor_tensor(out=mix[:, :, :], in0=mix[:, :, :], scalar=MIX, in1=mm01[:, :, :],
                                         op0=ALU.mult, op1=ALU.mult).then_inc(SEM["mix_ready"], 1)

            def score(g, i):
                for k in range(2 * i, 2 * i + 2):
                    dve.wait_ge(*filled("s_odd" if k % 2 else "s_even", i, g))
                    src = bank_of("s_odd" if k % 2 else "s_even", i)[:, :].rearrange("p (h n) -> p h n", n=N)
                    dve.tensor_reduce(smax[:, k, :], src, AX.X, ALU.max).then_inc(SEM["max_ready"], 1)
                    dve.wait_ge(*count("max_ready", g, k + 1))
                    dve.tensor_tensor(rows_of(unit(k)), src, wide(smax[:, k, :], N),
                                      ALU.subtract).then_inc(SEM["shift_ready"], 1)
                    if k > 0:
                        soft(g, k - 1)
                    if k == T - 1:
                        soft(g, k)

            def soft(g, k):
                u = unit(k)
                dve.wait_ge(*count("exp_ready", g, k + 1))
                dve.tensor_reduce(ssum[:, k, :], rows_of(u), AX.X, ALU.add).then_inc(SEM["sum_ready"], 1)
                dve.wait_ge(*count("sum_ready", g, k + 1))
                dve.tensor_scalar(ssc[:, k, :], ssum[:, k, :], 1.0 / MIX, None, ALU.mult).then_inc(SEM["rsum_ready"], 1)
                dve.wait_ge(*count("rsum_ready", g, 2 * k + 1))
                dve.reciprocal(srec[:, k, :], ssc[:, k, :]).then_inc(SEM["rsum_ready"], 1)
                dve.wait_ge(*count("rsum_ready", g, 2 * k + 2))
                dve.tensor_tensor(rows_of(u), rows_of(u), wide(srec[:, k, :], N), ALU.mult)\
                   .then_inc(SEM["prob_ready"], 1)
                dve.wait_ge(*count("prob_ready", g, k + 1))
                dve.wait_ge(*count("mix_ready", g, 1))
                t = k - k % 2
                dve.tensor_tensor(u, u, mix[:, t:t + 2, :].rearrange("p t (a n) -> p t a n", a=1)
                                  .broadcast_to([P, 2, HP, N]), ALU.add).then_inc(SEM["attn_ready"], 1)

            def out0(g, i):
                lo, hi = 2 * i, 2 * i + 2
                dve.wait_ge(*filled("out0", i, g))
                src = bank_of("out0", i)
                dve.wait_ge(*count("xb_ready", g, 1))
                ins = dve.tensor_tensor(flat(pre[0][:, lo:hi, :]), src[:, :], flat(xin[:, lo:hi, :]), ALU.add)
                ins.then_inc(SEM["sum0_ready"], 1)
                dve.wait_ge(*count("sum0_ready", g, i + 1))
                norm(g, 0, "0", pre[0], xl[0], lo, hi, "x1_ready")
                scale(g, 0, pre[0], xl[0], lo, hi, "x1_ready", i)

            def graph_a(g, i):
                dve.wait_ge(*count("adjB_in", g, 32))
                dve.tensor_scalar(edge[:, :, :], adjB[:, :, :], 0.0, None, ALU.not_equal).then_inc(SEM["edge_ready"], 1)
                dve.tensor_reduce(deg[:, :], adjB[:, :, :], AX.X, ALU.add).then_inc(SEM["deg_ready"], 1)
                dve.wait_ge(*count("deg_ready", g, 1))
                dve.tensor_scalar(degm[:, :], deg[:, :], 1e-6, None, ALU.max).then_inc(SEM["degmax"], 1)
                dve.wait_ge(*count("degmax", g, 1))
                dve.reciprocal(rdeg[:, :], degm[:, :]).then_inc(SEM["rdeg_ready"], 1)

            def graph_b(g, i):
                dve.wait_ge(*filled("cnt", 0, g))
                src = bank_of("cnt", 0)
                dve.tensor_scalar(cntm[:, :], src[:, 0:T], 1.0, None, ALU.max).then_inc(SEM["cntmax"], 1)
                dve.tensor_scalar(dpos[:, :], src[:, 2 * T:3 * T], 0.0, None, ALU.is_gt).then_inc(SEM["dsign"], 1)
                dve.tensor_scalar(dneg[:, :], src[:, 2 * T:3 * T], 0.0, None, ALU.is_le).then_inc(SEM["dsign"], 1)
                dve.wait_ge(*count("cntmax", g, 1))
                dve.reciprocal(be[:, :], cntm[:, :]).then_inc(SEM["be_ready"], 1)
                dve.wait_ge(*count("dsign", g, 2))
                ins = dve.scalar_tensor_tensor(out=dsafe[:, :], in0=src[:, 2 * T:3 * T], scalar=0.0, in1=dneg[:, :],
                                               op0=ALU.max, op1=ALU.add)
                ins.then_inc(SEM["dsafe"], 1)
                dve.wait_ge(*count("dsafe", g, 1))
                dve.reciprocal(drec[:, :], dsafe[:, :]).then_inc(SEM["drec"], 1)
                dve.wait_ge(*count("drec", g, 1))
                dve.tensor_tensor(dn[:, :], drec[:, :], dpos[:, :], ALU.mult).then_inc(SEM["dn_ready"], 1)

            def graph_c(g, i):
                dve.wait_ge(*filled("sym", 0, g))
                src = bank_of("sym", 0)
                dve.wait_ge(*count("dn_ready", g, 1))
                ins = dve.tensor_tensor(gmat[:, :, :], src[:, :].rearrange("p (t n) -> p t n", t=T),
                                        wide(dn[:, :], P), ALU.mult)
                ins.then_inc(SEM["g_ready"], 1)

            def mean(g, i):
                lo, hi = 2 * i, 2 * i + 2
                dve.wait_ge(*filled("mean", i, g))
                src = bank_of("mean", i)
                dve.wait_ge(*count("x1_ready", g, 2))
                ins = dve.scalar_tensor_tensor(out=flat(pre[1][:, lo:hi, :]), in0=src[:, :], scalar=0.0,
                                               in1=flat(xl[0][:, lo:hi, :]), op0=ALU.max, op1=ALU.add)
                ins.then_inc(SEM["sum1_ready"], 1)
                dve.wait_ge(*count("sum1_ready", g, i + 1))
                norm(g, 1, "1", pre[1], xl[1], lo, hi, "x2_ready")
                if i == 1:
                    dve.wait_ge(*count("out_done", g, 32, 1))
                    scale(g, 1, pre[1], xl[1], 0, 2, "x2_ready", 0)
                    scale(g, 1, pre[1], xl[1], 2, 4, "x2_ready", 1)

            def up(g, i):
                dve.wait_ge(*count("relu_ready", g, i + 1))
                norm(g, 4, "_h", r, r, i, i + 1, "h_ready")
                if i > 0:
                    scale(g, 4, r, r, i - 1, i, "h_ready", i - 1)
                if i == T - 1:
                    scale(g, 4, r, r, i, i + 1, "h_ready", i)

            def turn_h(g, i):
                if i >= 2:
                    dve.wait_ge(*filled("turn_h", i, g))
                    src = bank_of("turn_h", i)
                    ins = dve.tensor_scalar(hT[:, i, :], src[:, :], gam[:, i:i + 1], bet[:, i:i + 1], ALU.mult, ALU.add)
                    ins.then_inc(SEM["hT_dve"], 1)

            def hyper(g, i):
                for t in range(2 * i, 2 * i + 2):
                    dve.scalar_tensor_tensor(out=gate[:, t, :], in0=wd[:, :], scalar=deg[:, t:t + 1], in1=bd[:, :],
                                             op0=ALU.mult, op1=ALU.add).then_inc(SEM["z_ready"], 1)
                lo, hi = 2 * i, 2 * i + 2
                dve.wait_ge(*filled("hyper", i, g))
                src = bank_of("hyper", i)
                dve.wait_ge(*count("x2_ready", g, 2))
                ins = dve.scalar_tensor_tensor(out=flat(pre[1][:, lo:hi, :]), in0=flat(xl[1][:, lo:hi, :]), scalar=2.0,
                                               in1=src[:, :], op0=ALU.mult, op1=ALU.add)
                ins.then_inc(SEM["sum2_ready"], 1)
                dve.wait_ge(*count("sum2_ready", g, i + 1))
                norm(g, 2, "2", pre[1], xl[2], lo, hi, "x3_ready")
                if i == 1:
                    for k in range(2):
                        scale(g, 2, pre[1], xl[2], 2 * k, 2 * k + 2, "x3_ready", k)
                    for k in range(2):
                        dve.wait_ge(*count("x3_ready", g, k + 1))
                        dve.wait_ge(*count("gate_ready", g, k + 1))
                        dve.scalar_tensor_tensor(out=flat(xg[:, 2 * k:2 * k + 2, :]),
                                                 in0=flat(gate[:, 2 * k:2 * k + 2, :]), scalar=1.0,
                                                 in1=flat(xl[2][:, 2 * k:2 * k + 2, :]),
                                                 op0=ALU.add, op1=ALU.mult).then_inc(SEM["xg_ready"], 1)

            def simi(g, i):
                dve.wait_ge(*filled("sim", 0, g))
                src = bank_of("sim", 0)
                dve.wait_ge(*count("adjC_in", g, 32))
                ins = dve.tensor_tensor(flat(sim[:, :, :]), src[:, :], flat(adjC[:, :, :]), ALU.mult)
                ins.then_inc(SEM["sim_ready"], 1)
                dve.wait_ge(*count("sim_ready", g, 1))
                dve.tensor_reduce(simsum[:, :], sim[:, :, :], AX.X, ALU.add).then_inc(SEM["simsum"], 1)
                dve.wait_ge(*count("simsum", g, 1))
                dve.tensor_scalar(simeps[:, :], simsum[:, :], 64e-6, None, ALU.add).then_inc(SEM["simeps"], 1)
                dve.wait_ge(*count("simeps", g, 1))
                dve.reciprocal(simrec[:, :], simeps[:, :]).then_inc(SEM["simrec"], 1)
                dve.wait_ge(*count("simrec", g, 1))
                dve.tensor_tensor(smat[:, :, :], sim[:, :, :], wide(simrec[:, :], P), ALU.mult).then_inc(SEM["s_ready"], 1)

            def out3(g, i):
                lo, hi = 2 * i, 2 * i + 2
                dve.wait_ge(*filled("out3", i, g))
                src = bank_of("out3", i)
                ins = dve.scalar_tensor_tensor(out=flat(pre[1][:, lo:hi, :]), in0=src[:, :], scalar=0.0,
                                               in1=flat(xl[2][:, lo:hi, :]), op0=ALU.max, op1=ALU.add)
                ins.then_inc(SEM["sum3_ready"], 1)
                dve.wait_ge(*count("sum3_ready", g, i + 1))
                norm(g, 3, "3", pre[1], xl[3], lo, hi, "x4_ready")
                if i == 1:
                    scale(g, 3, pre[1], xl[3], 0, 2, "x4_ready", 0)
                    scale(g, 3, pre[1], xl[3], 2, 4, "x4_ready", 1)

            steps = {"mixmat": mixmat, "score": score, "out0": out0, "graph_a": graph_a, "graph_b": graph_b,
                     "graph_c": graph_c, "mean": mean, "up": up, "turn_h": turn_h, "hyper": hyper, "sim": simi,
                     "out3": out3}
            rounds(dve, lambda a, b: run(steps, a, b))

        @block.tensor
        def _(pe):
            pe.wait_ge(setup_dve, 12)

            def product(out_ap, pairs, bias=None):
                if bias is not None:
                    pe.matmul(out_ap, ones3[0:96, :], bias3[:, bias[0]:bias[1]], start=True, stop=False)
                for j, (l, rr) in enumerate(pairs):
                    ins = pe.matmul(out_ap, l, rr, start=(bias is None and j == 0), stop=(j == len(pairs) - 1))
                return ins

            def tile_of(ap, c, t):
                return ap[:, c, t * P:(t + 1) * P]

            def mixmat(g, i):
                pe.wait_ge(*emptied("mixmat", 0, g))
                dst = bank_of("mixmat", 0)
                apart(pe, g)
                for t in range(T):
                    ins = pe.matmul(dst[:, t * N:(t + 1) * N], mi_tile(g, t), mj_tile(g, t),
                                    start=True, stop=True)
                now_full(ins, "mixmat", 0)

            def mi_tile(g, t):
                return mi[:, bass.ds(g * T + t, 1), :].rearrange("p a n -> p (a n)")

            def mj_tile(g, t):
                return mj[:, bass.ds(g * T + t, 1), :].rearrange("p a n -> p (a n)")

            def proj(name, w, g, i):
                pe.wait_ge(*count("xT_in", g, 32))
                pe.wait_ge(*emptied(name, i, g))
                dst = bank_of(name, i)
                now_full(product(dst[:, :], [(w[:, c, i * P:(i + 1) * P], xT[:, c, :]) for c in range(C)]), name, i)

            def val(g, i):
                pe.wait_ge(*emptied("v", i, g))
                dst = bank_of("v", i)
                now_full(product(dst[:, :], [(tile_of(xT, c, i), wv[:, c, :]) for c in range(C)]), "v", i)

            def score(g, i):
                pe.wait_ge(*count("q_ready", g, HP))
                pe.wait_ge(*count("k_ready", g, HP))
                pe.wait_ge(*emptied("s_odd", i, g))
                dst = [bank_of("s_even", i), bank_of("s_odd", i)]
                apart(pe, g)
                for e in range(2):
                    for k in range(2):
                        pe.matmul(dst[e][:, k * HP * N:(k + 1) * HP * N], mi_tile(g, 2 * i + k),
                                  mj[:, bass.ds(g * T + 2 * i + k, 1), :].broadcast_to([4, HP, N]),
                                  start=(k == 0), stop=False, skip_group_check=True)
                ins = None
                for k in range(2):
                    for p in range(HP):
                        for gr in range(2):
                            for e in range(2):
                                tok = slice((2 * i + k) * P + gr * N, (2 * i + k) * P + (gr + 1) * N)
                                col = (k * HP + p) * N
                                ins0, ins = ins, pe.matmul(dst[e][gr * N:(gr + 1) * N, col:col + N],
                                                qT[e * DH:(e + 1) * DH, p, tok], kT[e * DH:(e + 1) * DH, p, tok],
                                                start=False, stop=(k == 1 and p == HP - 1), skip_group_check=True)
                now_full(ins0, "s_even", i)
                now_full(ins, "s_odd", i)

            def head(g, i):
                pe.wait_ge(*count("attn_ready", g, i - i % 2 + 2))
                pe.wait_ge(*emptied("pT", i, g))
                dst = bank_of("pT", i)
                for p in range(HP):
                    ins = pe.transpose(dst[:, p * P:(p + 1) * P],
                                       prob[:, i, p].rearrange("p e n -> p (e n)"), ident[:, :])
                now_full(ins, "pT", i)
                pe.wait_ge(*count("pT_ready", g, i + 1))
                pe.wait_ge(*count("v_ready", g, i + 1))
                pe.wait_ge(*emptied("oT", i, g))
                dst = bank_of("oT", i)
                apart(pe, g)
                for p in range(HP):
                    for gr in range(2):
                        for e in range(2):
                            rows = slice(e * N, (e + 1) * N)
                            ins = pe.matmul(dst[rows, p * P + gr * N:p * P + (gr + 1) * N], v[rows, i, gr, p, :],
                                            pT[rows, i % 2, p, gr * N:(gr + 1) * N], start=True, stop=True,
                                            skip_group_check=True)
                now_full(ins, "oT", i)

            def two_tiles(name, i, pairs_of, bias=None):
                dst = bank_of(name, i)
                for k in range(2):
                    ins = product(dst[:, k * D:(k + 1) * D], pairs_of(2 * i + k), bias)
                now_full(ins, name, i)

            def out0(g, i):
                pe.wait_ge(*count("oT_ready", g, 2 * i + 2))
                pe.wait_ge(*emptied("out0", i, g))
                two_tiles("out0", i, lambda t: [(tile_of(oT, p, t), wo[:, p, :]) for p in range(HP)])

            def turned(name, g, i, src, ready, n):
                pe.wait_ge(*count(ready, g, n))
                pe.wait_ge(*emptied(name, i, g))
                dst = bank_of(name, i)
                for t in range(T):
                    ins = pe.transpose(dst[:, t * P:(t + 1) * P], src[:, t, i * P:(i + 1) * P], ident[:, :])
                now_full(ins, name, i)

            def graph_a(g, i):
                pe.wait_ge(*count("edge_ready", g, 1))
                pe.wait_ge(*emptied("ht", 0, g))
                dst = bank_of("ht", 0)[:, 0:T * P // 2].bitcast(BF16)
                for t in range(T):
                    ins = pe.transpose(dst[:, t * P:(t + 1) * P], edge[:, t, :], identb[:, :])
                now_full(ins, "ht", 0)

            def graph_b(g, i):
                pe.wait_ge(*count("ht_ready", g, 1))
                pe.wait_ge(*emptied("cnt", 0, g))
                dst = bank_of("cnt", 0)
                for t in range(T):
                    pe.matmul(dst[:, t:t + 1], edge[:, t, :], onescol[:, 0:1], start=True, stop=True)
                for t in range(T):
                    ins = pe.matmul(dst[:, 2 * T + t:2 * T + t + 1], hT0[:, t, :],
                                    row0[:, bass.ds(g * T + t, 1)], start=True, stop=True)
                now_full(ins, "cnt", 0)

            def graph_c(g, i):
                pe.wait_ge(*count("bht_ready", g, 1))
                pe.wait_ge(*emptied("sym", 0, g))
                dst = bank_of("sym", 0)
                for t in range(T):
                    ins = pe.matmul(dst[:, t * P:(t + 1) * P], hT0[:, t, :], bhT[:, t, :], start=True, stop=True)
                now_full(ins, "sym", 0)
                pe.wait_ge(*count("meanA_ready", g, 1))
                pe.wait_ge(*emptied("meanT", 0, g))
                dst = bank_of("meanT", 0)
                for t in range(T):
                    ins = pe.transpose(dst[:, t * P:(t + 1) * P], meanA[:, t, :], ident[:, :])
                now_full(ins, "meanT", 0)

            def graph_d(g, i):
                pe.wait_ge(*count("g_ready", g, 1))
                pe.wait_ge(*emptied("gT", 0, g))
                dst = bank_of("gT", 0)
                for t in range(T):
                    ins = pe.transpose(dst[:, t * P:(t + 1) * P], gmat[:, t, :], ident[:, :])
                now_full(ins, "gT", 0)

            def gathered(name, g, i, src, mat):
                pe.wait_ge(*emptied(name, i, g))
                dst = bank_of(name, i)
                for t in range(T):
                    ins = pe.matmul(dst[:, t * P:(t + 1) * P], src[:, t, i * P:(i + 1) * P], mat[:, t, :],
                                    start=True, stop=True)
                now_full(ins, name, i)

            def agg(g, i):
                pe.wait_ge(*count("meanT_ready", g, 1))
                gathered("agg", g, i, xl[0], meanT)

            def mean(g, i):
                pe.wait_ge(*count("turn1_ready", g, 2))
                pe.wait_ge(*count("agg_ready", g, 2))
                two_tiles("mean", i, lambda t: [(tile_of(x1T, c, t), wm[:, c, :]) for c in range(C)]
                          + [(tile_of(aggT, c, t), wm[:, C + c, :]) for c in range(C)])

            def spread(g, i):
                pe.wait_ge(*count("x2_ready", g, 2))
                pe.wait_ge(*count("gT_ready", g, 1))
                gathered("spread", g, i, xl[1], gT)

            def up(g, i):
                pe.wait_ge(*count("spread_ready", g, 2))
                pe.wait_ge(*emptied("up", i, g))
                dst = bank_of("up", i)
                now_full(product(dst[:, :], [(tile_of(spT, c, i), w1[:, c, :]) for c in range(C)], (0, HID)), "up", i)

            def down(g, i):
                pe.wait_ge(*count("hT_act", g, 2))
                pe.wait_ge(*count("hT_dve", g, 2))
                pe.wait_ge(*emptied("down", i, g))
                two_tiles("down", i, lambda t: [(tile_of(hT, c, t), w2[:, c, :]) for c in range(HC)])

            def hyper(g, i):
                pe.wait_ge(*count("down_ready", g, i + 1))
                pe.wait_ge(*emptied("hyper", i, g))
                two_tiles("hyper", i, lambda t: [(gT[:, t, :], yw[:, t, :])], (HID, HID + D))

            def qk(g, i):
                pe.wait_ge(*count("turn3_ready", g, 2))
                pe.wait_ge(*emptied("qk", i, g))
                dst = bank_of("qk", i)
                now_full(product(dst[:, :], [(wqk[:, c, i * P:(i + 1) * P], xgT[:, c, :]) for c in range(C)]), "qk", i)

            def simi(g, i):
                pe.wait_ge(*count("qk_ready", g, 2))
                pe.wait_ge(*emptied("sim", 0, g))
                dst = bank_of("sim", 0)
                for t in range(T):
                    ins = product(dst[:, t * P:(t + 1) * P], [(tile_of(qkT, c, t), tile_of(qkT, c, t)) for c in range(C)])
                now_full(ins, "sim", 0)

            def turn_s(g, i):
                pe.wait_ge(*count("s_ready", g, 1))
                pe.wait_ge(*emptied("turn_s", 0, g))
                dst = bank_of("turn_s", 0)
                for t in range(T):
                    ins = pe.transpose(dst[:, t * P:(t + 1) * P], smat[:, t, :], ident[:, :])
                now_full(ins, "turn_s", 0)

            def agg3_(g, i):
                pe.wait_ge(*count("sT_ready", g, 1))
                gathered("agg3", g, i, xg, sT)

            def out3(g, i):
                pe.wait_ge(*count("agg3_ready", g, 2))
                pe.wait_ge(*emptied("out3", i, g))
                two_tiles("out3", i, lambda t: [(tile_of(agg3, c, t), wlr[:, c, :]) for c in range(C)]
                          + [(tile_of(xgT, c, t), wlr[:, C + c, :]) for c in range(C)], (HID + D, HID + 2 * D))

            steps = {
                "mixmat": mixmat, "q": lambda g, i: proj("q", wq, g, i), "k": lambda g, i: proj("k", wk, g, i),
                "v": val, "score": score, "head": head, "out0": out0,
                "turn1": lambda g, i: turned("turn1", g, i, xl[0], "x1_ready", 2),
                "graph_a": graph_a, "graph_b": graph_b, "graph_c": graph_c, "graph_d": graph_d, "agg": agg,
                "mean": mean, "spread": spread, "up": up,
                "turn_h": lambda g, i: turned("turn_h", g, i, r, "h_ready", T),
                "down": down, "hyper": hyper,
                "turn3": lambda g, i: turned("turn3", g, i, xg, "xg_ready", 2),
                "qk": qk, "sim": simi, "turn_s": turn_s, "agg3": agg3_, "out3": out3,
            }
            rounds(pe, lambda a, b: run(steps, a, b))


def kernel(**inputs):
    import numpy as _np
    import concourse.bacc as _bacc
    from concourse import mybir as _mybir
    from concourse.bass_utils import run_bass_kernel_spmd as _run

    a = {k: _np.asarray(v) for k, v in inputs.items()}
    ident = _np.eye(P, dtype=_np.float32)
    ones3 = _np.zeros((P, P), _np.float32)
    ones3[[0, 32, 64]] = 1.0
    mrow = _np.zeros((4, 1 + P), _np.float32)
    mrow[:, 0] = [1, 0, 1, 0]
    mrow[0:2, 1:1 + N] = [[-BIG], [BIG]]
    mrow[2:4, 1 + N:] = [[-BIG], [BIG]]
    arrays = {
        "x": a["x"], "x_t": a["x"].reshape(B * N, D).T, "adj": a["adj"],
        "adj_row0": a["adj"][:, 0, :].reshape(B // 2, P).T, "mask_u8": a["nodemask"],
        "wqkv": a["L0_gnn_W_qkv"], "w_out": a["L0_gnn_W_out"], "b_out": a["L0_gnn_b_out"],
        "w_mean_t": a["L1_gnn_W"].T, "w1_t": a["L2_gnn_W1"].T, "b1": a["L2_gnn_b1"],
        "gamma_c": a["L2_gnn_gamma"].reshape(HC, P).T, "beta_c": a["L2_gnn_beta"].reshape(HC, P).T,
        "w2_t": a["L2_gnn_W2"].T, "b2": a["L2_gnn_b2"], "wqk_t": a["L3_gnn_Wqk"].T,
        "bqk_c": a["L3_gnn_bqk"].reshape(C, P).T, "wl_t": a["L3_gnn_Wl"].T, "bl": a["L3_gnn_bl"],
        "wr_t": a["L3_gnn_Wr"].T, "wd_r": a["L3_gnn_Wd"].reshape(D), "bd_r": a["L3_gnn_bd"],
        "ident_c": ident, "ones3_c": ones3, "mrow_c": mrow,
    }
    nc = _bacc.Bacc("TRN2", target_bir_lowering=False, num_devices=1)
    maps, args = {}, []
    for name, arr in arrays.items():
        arr = _np.ascontiguousarray(arr)
        maps[f"in_{name}"] = arr
        args.append(nc.dram_tensor(f"in_{name}", arr.shape, _mybir.dt.from_np(arr.dtype), kind="ExternalInput").ap())
    out = nc.dram_tensor("out_x", (B, N, D), F32, kind="ExternalOutput").ap()
    graph_layers(nc, *args, out)
    r = _run(nc, [maps], core_ids=[0])
    return r.results[0]["out_x"]
```

```python
from contextlib import ExitStack

import concourse.bass as bass
from concourse import mybir

ALU = mybir.AluOpType
ACT = mybir.ActivationFunctionType
AX = mybir.AxisListType
F32 = mybir.dt.float32
F32R = mybir.dt.float32r
BF16 = mybir.dt.bfloat16
U8 = mybir.dt.uint8

P = 128
N = 64
D = 256
B = 128
H = 8
DH = 64
HID = 512
T = 4
GRP = B * N // (T * P)
TOK = T * P
C = D // P
HP = H // 2
HC = HID // P
NBIAS = HID + 3 * D
EPS_LN = 1e-5
MIX = 0.33
BIG = 2.0 ** 120

SCHEDULE = [
    ("B", "turn1", 0), ("B", "turn1", 1), ("A", "k", 1), ("B", "graph_a", 0), ("C", "scale3", 0), ("A", "k", 2),
    ("B", "graph_b", 0), ("B", "graph_m", 0), ("A", "mask", 0), ("A", "k", 3), ("B", "agg", 0), ("B", "agg", 1),
    ("B", "graph_c", 0), ("A", "mixmat", 0), ("A", "score", 0), ("A", "shift", 0), ("B", "graph_d", 0),
    ("A", "shift", 1), ("B", "mean", 0), ("B", "mean", 1), ("A", "v", 0), ("B", "scale1", 0), ("A", "v", 1),
    ("A", "v", 2), ("A", "soft", 0), ("A", "soft", 1), ("B", "spread", 0), ("B", "spread", 1), ("A", "v", 3),
    ("B", "up", 0), ("B", "up", 1), ("B", "up", 2), ("B", "up", 3), ("A", "score", 1),
    ("B", "turn_h", 0), ("B", "turn_h", 1), ("B", "turn_h", 2), ("B", "turn_h", 3), ("B", "gate", 0),
    ("A", "shift", 2), ("A", "shift", 3), ("N", "split", 0), ("A", "turnp", 0), ("A", "turnp", 1),
    ("B", "down", 0), ("A", "soft", 2), ("B", "down", 1), ("A", "soft", 3), ("A", "pv", 0), ("B", "hyper", 0),
    ("A", "pv", 1), ("B", "hyper", 1), ("N", "split_low", 0), ("B", "gated", 0), ("A", "turnp", 2), ("A", "turnp", 3),
    ("B", "gated", 1), ("A", "out0", 0), ("A", "pv", 2), ("A", "pv", 3), ("A", "scale0", 0),
    ("B", "turn3", 0), ("B", "turn3", 1), ("N", "q", 0), ("B", "qk", 0), ("B", "qk", 1), ("A", "out0", 1),
    ("B", "sim", 0), ("A", "scale0", 1), ("N", "q", 1), ("N", "q", 2), ("B", "turn_s", 0), ("N", "q", 3),
    ("B", "agg3", 0), ("B", "agg3", 1), ("N", "k", 0), ("B", "out3", 0), ("B", "out3", 1),
]

FILLS = {"graph_a": ["ht"], "graph_b": ["cnt"], "graph_c": ["sym"], "graph_m": ["meanT"], "graph_d": ["gT"],
         "score": ["s_even", "s_odd"], "turnp": ["pT"], "pv": ["oT"],
         "split": [], "split_low": [], "mask": [], "shift": [], "soft": [], "gate": [],
         "gated": [], "scale0": [], "scale1": [], "scale3": []}
BANK = {}
PER_BANK = [0] * 8
_turn = {True: 0, False: 4}
_order = []
for _s, _n, _i in SCHEDULE:
    for _f in FILLS.get(_n, [_n]):
        _order.append((_turn[_s != "B"], _s == "N", _f, _i))
        _turn[_s != "B"] = (_turn[_s != "B"] + 1) % 4 + (4 if _s == "B" else 0)
for _k in range(8):
    _here = [x for x in _order if x[0] == _k]
    assert [x[1] for x in _here] == sorted(x[1] for x in _here)
    for _, _, _f, _i in sorted(_here, key=lambda x: not x[1]):
        BANK[(_f, _i)] = (_k, PER_BANK[_k])
        PER_BANK[_k] += 1

BEFORE = {}
for _key, (_b, _c) in BANK.items():
    _prev = (_c - 1) % PER_BANK[_b]
    BEFORE[_key] = (_b, next(k for k, v in BANK.items() if v == (_b, _prev)), 1 if _c == 0 else 0)
READ_OUT = {
    "mixmat": "mm_ready", "q": "q_ready", "k": "k_ready", "v": "v_ready", "pT": "pT_ready", "oT": "oT_lo",
    "out0": "sum0_ready", "turn1": "turn1_lo", "agg": "agg_lo", "mean": "sum1_ready", "ht": "ht_ready",
    "cnt": "dsafe", "sym": "g_ready", "meanT": "meanT_ready", "gT": "gT_ready", "spread": "spread_lo",
    "up": "relu_ready", "turn_h": "hT_lo", "down": "down_ready", "hyper": "sum2_ready", "turn3": "turn3_lo",
    "qk": "qk_tanh", "sim": "sim_ready", "turn_s": "sT_ready", "agg3": "agg3_lo", "out3": "sum3_ready",
}


PER = {
    "xT_in": 32, "x_in": 16, "adjA_in": 16, "adjB_in": 32, "mask_in": 16, "out_done": 32, "xT_hi": 2, "xT_lo": 2, "mask_rows": 2,
    "xb_ready": 1, "expA_ready": 1, "mm_ready": 1, "mix_sum": 1, "mix_ready": 1,
    "q_ready": 4, "k_ready": 4, "v_ready": 4,
    "max_ready": 4, "shift_ready": 4, "exp_ready": 4, "sum_ready": 4, "rsum_ready": 4, "prob_ready": 4,
    "attn_ready": 4, "pT_ready": 4, "oT_hi": 4, "oT_lo": 4,
    "sum0_ready": 2, "stats0": 4, "mv0": 4, "var0": 2, "rstd0": 2, "x1_ready": 2,
    "turn1_hi": 2, "turn1_lo": 2, "agg_hi": 2, "agg_lo": 2,
    "edge_ready": 1, "deg_ready": 1, "degmax": 1, "rdeg_ready": 1, "meanA_ready": 1, "ht_ready": 1,
    "cntmax": 1, "be_ready": 1, "bht_ready": 1, "dsign": 2, "dsafe": 1, "drec": 1, "dn_ready": 1,
    "g_ready": 1, "meanT_ready": 1, "gT_ready": 1,
    "sum1_ready": 2, "stats1": 4, "mv1": 4, "var1": 2, "rstd1": 2, "x2_ready": 2,
    "spread_hi": 2, "spread_lo": 2, "relu_ready": 4, "stats_h": 4, "mv_h": 4, "var_h": 4, "rstd_h": 4, "h_ready": 4,
    "hT_hi": 4, "hT_lo": 4, "down_ready": 2,
    "sum2_ready": 2, "stats2": 4, "mv2": 4, "var2": 2, "rstd2": 2, "x3_ready": 2,
    "z_ready": 2, "gate_ready": 2, "xg_ready": 2, "turn3_hi": 2, "turn3_lo": 2, "qk_tanh": 2, "qk_ready": 2,
    "sim_ready": 1, "simsum": 1, "simeps": 1, "simrec": 1, "s_ready": 1, "sT_ready": 1, "agg3_hi": 2, "agg3_lo": 2,
    "sum3_ready": 2, "stats3": 4, "mv3": 4, "var3": 2, "rstd3": 2, "x4_ready": 2,
}


def graph_layers(nc, x, x_t, adj, adj_row0, mask_rows, wqkv, w_out, b_out, w_mean_t, w1_t, b1, gamma_c, beta_c, w2_t, b2,
                 wqk_t, bqk_c, wl_t, bl, wr_t, wd_r, bd_r, ident_c, ones3_c, mrow_c, out):
    with ExitStack() as ctx:
        def sb(name, shape, dt=F32):
            return ctx.enter_context(nc.sbuf_tensor(name, shape, dt))

        def split(name, shape):
            return [sb(name + "_hi", shape, F32R), sb(name + "_lo", shape, F32R)]

        def part(pair, *at):
            return [p[at] for p in pair]

        wq = split("wq", [P, C, H * DH])
        wk = split("wk", [P, C, H * DH])
        wv = split("wv", [P, C, H * DH])
        wo = split("wo", [P, HP, D])
        wm = split("wm", [P, 2 * C, D])
        w1 = split("w1", [P, C, HID])
        w2 = split("w2", [P, HC, D])
        wqk = split("wqk", [P, C, D])
        wlr = split("wlr", [P, 2 * C, D])
        ident = sb("ident", [P, P])
        identb = sb("identb", [P, P], BF16)
        onesf = sb("onesf", [P, P])
        ones3 = sb("ones3", [P, P], BF16)
        onescol = sb("onescol", [P, 2], BF16)
        bias3 = sb("bias3", [96, NBIAS], BF16)
        bout = sb("bout", [P, D])
        wd = sb("wd", [P, D])
        bd = sb("bd", [P, D])
        gam = sb("gam", [P, HC])
        bet = sb("bet", [P, HC])
        bqk = sb("bqk", [P, C])
        row0 = sb("row0", [P, T * GRP])
        negh = sb("negh", [P, T])
        mcst = sb("mcst", [4, 1 + P])
        masks = sb("masks", [4, T * (P + N)], U8)
        mi = sb("mi", [4, T, P], BF16)
        mj = sb("mj", [4, T, N], BF16)
        xTin = sb("xTin", [P, C, TOK])
        xT = split("xT", [P, C, TOK])
        xin = sb("xin", [P, T, D])
        adjA = sb("adjA", [P, T, N])
        expA = sb("expA", [P, T, N])
        mm01 = sb("mm01", [P, T, N])
        mix = sb("mix", [P, T, N])
        qT = sb("qT", [P, HP, TOK])
        kT = sb("kT", [P, HP, TOK])
        v = sb("v", [P, T, 2, HP, DH])
        prob = sb("prob", [P, T, HP, 2, N])
        smax = sb("smax", [P, T, 2 * HP])
        ssum = sb("ssum", [P, T, 2 * HP])
        srec = sb("srec", [P, T, 2 * HP])
        pT = sb("pT", [P, 2, HP, P])
        oT = split("oT", [P, HP, 2 * P])
        adjB = sb("adjB", [P, T, P])
        edge = sb("edge", [P, T, P], BF16)
        deg = sb("deg", [P, T])
        degm = sb("degm", [P, T])
        rdeg = sb("rdeg", [P, T])
        meanA = sb("meanA", [P, T, P])
        meanT = sb("meanT", [P, T, P])
        hT0 = sb("hT0", [P, T, P])
        bhT = sb("bhT", [P, T, P])
        cntm = sb("cntm", [P, T])
        be = sb("be", [P, T])
        dpos = sb("dpos", [P, T])
        dneg = sb("dneg", [P, T])
        dsafe = sb("dsafe", [P, T])
        drec = sb("drec", [P, T])
        dn = sb("dn", [P, T])
        gmat = sb("gmat", [P, T, P])
        gT = sb("gT", [P, T, P])
        hT = split("hT", [P, HC, TOK])
        x1T = part(hT, slice(None), slice(0, C))
        aggT = part(hT, slice(None), slice(C, 2 * C))
        agg3 = aggT
        spT = split("spT", [P, C, TOK])
        xgT = spT
        r = sb("r", [P, T, HID])
        qkT = r[:, 0:C, :]
        yw = sb("yw", [P, T, D])
        gate = r[:, C:2 * C, :].rearrange("p a (b d) -> p (a b) d", d=D)
        xg = yw
        sim = hT0
        smat = sim
        sT = bhT
        simsum = sb("simsum", [P, T])
        simeps = sb("simeps", [P, T])
        simrec = sb("simrec", [P, T])
        xl = [sb(f"x{i + 1}", [P, T, D]) for i in range(3)]
        xl.append(xl[1])
        stats = [sb(f"stats{i}", [P, T, 6]) for i in range(5)]
        mv = [sb(f"mv{i}", [P, T, 2]) for i in range(5)]
        var = [sb(f"var{i}", [P, T]) for i in range(5)]
        rstd = [sb(f"rstd{i}", [P, T]) for i in range(5)]

        def lent(ap, n, m):
            return ap.rearrange("p (c n) -> p c n", n=m)[:, 0:n, :]

        def flat(ap):
            return ap.rearrange("p t n -> p (t n)")

        raw_q, raw_k, raw_v = r[:, 0:2, :], r[:, 2:4, :], lent(flat(xl[1][:, :, :]), C, HID)
        raw_o, raw_m, raw_1 = xl[2][:, :, :], yw[:, :, :], lent(flat(xl[0][:, :, :]), C, HID)
        raw_2, raw_lr = lent(flat(raw_q), HC, D), lent(flat(raw_k), HC, D)
        raw_qk = lent(flat(hT0[:, :, :]), C, D)
        b1row, b2row = flat(bhT[0:1, :, :]), flat(meanA[0:1, :, :])
        trow = flat(meanT[0:1, :, :])[:, 0:D]
        rem = [flat(gmat[0:1, :, :]), flat(gT[0:1, :, :])]

        bank = [ctx.enter_context(nc.psum_tensor(f"bank{i}", [P, 512], F32)) for i in range(8)]
        SEM = {n: ctx.enter_context(nc.semaphore(n)) for n in PER}
        full = [ctx.enter_context(nc.semaphore(f"bank{i}_full")) for i in range(8)]
        weights_in = ctx.enter_context(nc.semaphore("weights_in"))
        qkv_in = [ctx.enter_context(nc.semaphore(f"{n}_weights_in")) for n in "qkv"]
        bias_in = ctx.enter_context(nc.semaphore("bias_in"))
        t_full = ctx.enter_context(nc.semaphore("t_full"))
        t_ready = ctx.enter_context(nc.semaphore("t_ready"))
        bias_ready = ctx.enter_context(nc.semaphore("bias_ready"))
        weights_ready = ctx.enter_context(nc.semaphore("weights_ready"))
        early_in = ctx.enter_context(nc.semaphore("early_in"))
        zero_ready = ctx.enter_context(nc.semaphore("zero_ready"))
        parted = ctx.enter_context(nc.semaphore("parted"))
        setup_dve = ctx.enter_context(nc.semaphore("setup_dve"))

        def count(sem, g, k, back=0):
            n = g * PER[sem] + (k - back * PER[sem])
            return (zero_ready, 4) if isinstance(n, int) and n <= 0 else (SEM[sem], n)

        def apart(eng, g):
            if not isinstance(g, int):
                eng.sem_inc(parted, 1)

        def unit(k):
            return prob[:, k - k % 2:k - k % 2 + 2, :, k % 2, :]

        def rows_of(ap):
            return ap.rearrange("p t h n -> p (t h) n")

        def bank_of(fill, i):
            return bank[BANK[(fill, i)][0]]

        def filled(fill, i, g, back=0):
            b, c = BANK[(fill, i)]
            n = g * PER_BANK[b] + (c + 1 - back * PER_BANK[b])
            return (zero_ready, 4) if isinstance(n, int) and n <= 0 else (full[b], n)

        def emptied(fill, i, g):
            b, (f, j), back = BEFORE[(fill, i)]
            if f in ("s_even", "s_odd"):
                return count("shift_ready", g, 2 * j + 1 + (f == "s_odd"), back)
            return count(READ_OUT[f], g, j + 1, back)

        def now_full(ins, fill, i):
            ins.then_inc(full[BANK[(fill, i)][0]], 1)

        def rounds(eng, body):
            body(0, None, None, None)
            body(1, 0, None, None)
            body(2, 1, 0, None)
            with eng.Fori(1, GRP - 2) as g:
                body(g + 2, g + 1, g, g - 1)
            body(None, GRP - 1, GRP - 2, GRP - 3)
            body(None, None, GRP - 1, GRP - 2)
            body(None, None, None, GRP - 1)

        def run(steps, n, a, b, c):
            group = {"N": n, "A": a, "B": b, "C": c}
            for stream, name, i in SCHEDULE:
                if group[stream] is not None and name in steps:
                    steps[name](group[stream], i)

        x_g = x.rearrange("(g t h) n d -> g (h n) t d", t=T, h=2)
        out_g = out.rearrange("(g t h) n d -> g (h n) t d", t=T, h=2)
        xT_g = x_t.rearrange("(c p) (g n) -> g p c n", p=P, n=TOK)
        adj_g = adj.rearrange("(g t h) n m -> g (h n) t m", t=T, h=2)
        adj_h = adj.rearrange("(g t h) n m -> g h n t m", t=T, h=2)
        mask_g = mask_rows.rearrange("a (g n) -> g a n", n=T * (P + N))

        block = ctx.enter_context(nc.Block())

        @block.sync
        def _(sp):
            sp.dma_start(mcst[:, :], mrow_c).then_inc(early_in, 16)
            sp.dma_start(ident[:, :], ident_c).then_inc(early_in, 16)
            sp.dma_start(onesf[:, :], ones3_c).then_inc(early_in, 16)
            wqkv_v = wqkv.rearrange("(c k) (h i d) -> i c k h d", k=P, h=H, i=3)

            def load(n, a, b):
                if n is not None:
                    sp.wait_ge(*count("xT_lo", n, 2, 1))
                    for c in range(C):
                        sp.dma_start(xTin[:, c, :], xT_g[n][:, c, :]).then_inc(SEM["xT_in"], 16)
                if a is not None:
                    sp.wait_ge(*count("mask_rows", a, 2, 1))
                    apart(sp, a)
                    sp.dma_start(masks[:, :], mask_g[a]).then_inc(SEM["mask_in"], 16)
                    sp.wait_ge(*count("mix_sum", a, 1, 1))
                    sp.dma_start(adjA[:, :, :], adj_g[a]).then_inc(SEM["adjA_in"], 16)
                    sp.wait_ge(*count("sum0_ready", a, 2, 1))
                    sp.dma_start(xin[:, :, :], x_g[a]).then_inc(SEM["x_in"], 16)
                if b is not None:
                    sp.wait_ge(*count("meanA_ready", b, 1, 1))
                    sp.wait_ge(*count("sim_ready", b, 1, 1))
                    if isinstance(b, int) and b == 0:
                        sp.wait_ge(zero_ready, 1)
                    for h in range(2):
                        sp.dma_start(adjB[h * N:(h + 1) * N, :, h * N:(h + 1) * N],
                                     adj_h[b, h]).then_inc(SEM["adjB_in"], 16)

            def store(b):
                for i in range(2):
                    sp.wait_ge(*count("x4_ready", b, i + 1))
                    sp.dma_start(out_g[b][:, 2 * i:2 * i + 2, :], xl[3][:, 2 * i:2 * i + 2, :]).then_inc(SEM["out_done"], 16)

            load(0, None, None)
            def matrix(dst, src):
                sp.dma_start(dst, src.rearrange("(c k) n -> k c n", k=P)).then_inc(weights_in, 16)

            for i, w in enumerate((raw_q, raw_k, raw_v)):
                for c in range(C):
                    sp.dma_start(w[:, c, :].rearrange("p (h d) -> p h d", h=H), wqkv_v[i, c]).then_inc(qkv_in[i], 16)
            matrix(raw_o, w_out)
            matrix(raw_1, w1_t)
            sp.wait_ge(weights_ready, 1)
            matrix(raw_2, w2_t)
            matrix(raw_m, w_mean_t)
            matrix(raw_qk, wqk_t)
            sp.wait_ge(weights_ready, 2)
            matrix(raw_lr[:, 0:C, :], wl_t)
            matrix(raw_lr[:, C:2 * C, :], wr_t)
            sp.dma_start(bqk[:, :], bqk_c).then_inc(weights_in, 16)
            sp.dma_start(row0[:, :], adj_row0).then_inc(weights_in, 16)
            load(1, 0, None)
            load(2, 1, 0)
            with sp.Fori(1, GRP - 2) as g:
                load(g + 2, g + 1, g)
                store(g - 1)
            load(None, GRP - 1, GRP - 2)
            store(GRP - 3)
            load(None, None, GRP - 1)
            store(GRP - 2)
            store(GRP - 1)
            sp.wait_ge(*count("out_done", GRP - 1, 32))

        @block.gpsimd
        def _(pool):
            pool.memset(adjB[:, :, :], 0.0).then_inc(zero_ready, 1)
            pool.memset(negh[:, :], -0.5).then_inc(zero_ready, 1)
            pool.memset(bias3[:, :], 0.0).then_inc(zero_ready, 1)
            pool.memset(onescol[:, :], 1.0).then_inc(zero_ready, 1)
            pool.wait_ge(zero_ready, 4)

            split_steps = [0]

            def bias_parts(src, lo, n):
                at = slice(lo, lo + n)
                first, second = rem[0][:, 0:n], rem[1][:, 0:n]
                before = split_steps[0]
                split_steps[0] += 6
                pool.tensor_copy(bias3[0:1, at], src).then_inc(bias_ready, 1)
                pool.wait_ge(bias_ready, before + 1)
                pool.tensor_tensor(first, src, bias3[0:1, at], ALU.subtract).then_inc(bias_ready, 1)
                pool.wait_ge(bias_ready, before + 2)
                pool.tensor_copy(bias3[32:33, at], first).then_inc(bias_ready, 1)
                pool.wait_ge(bias_ready, before + 3)
                pool.tensor_copy(second, bias3[32:33, at]).then_inc(bias_ready, 1)
                pool.wait_ge(bias_ready, before + 4)
                pool.tensor_tensor(second, first, second, ALU.subtract).then_inc(bias_ready, 1)
                pool.wait_ge(bias_ready, before + 5)
                pool.tensor_copy(bias3[64:65, at], second).then_inc(bias_ready, 1)
                pool.wait_ge(bias_ready, before + 6)

            def biases(g, i):
                if isinstance(g, int) and g == 0 and i == 0:
                    pool.wait_ge(bias_in, 16 * 8)
                    bias_parts(b1row, 0, HID)
                    bias_parts(b2row, HID, 2 * D)
                if isinstance(g, int) and g == 0 and i == 3:
                    pool.wait_ge(t_ready, 1)
                    bias_parts(trow, HID + 2 * D, D)

            def residual(g, i):
                if isinstance(g, int) and g == 0:
                    pool.wait_ge(bias_in, 16 * 8)
                pool.wait_ge(*count("x_in", g, 16))
                pool.tensor_tensor(xin[:, :, :], xin[:, :, :],
                                   bout[:, :].rearrange("p (a d) -> p a d", a=1).broadcast_to([P, T, D]),
                                   ALU.add).then_inc(SEM["xb_ready"], 1)

            def inv_root(g, layer, name, lo, hi, k):
                pool.wait_ge(*count(f"mv{name}", g, hi))
                n = "_h" if layer == 4 else str(layer)
                apart(pool, g)
                pool.tensor_scalar(var[layer][:, lo:hi], mv[layer][:, lo:hi, 1], EPS_LN, None,
                                   ALU.add).then_inc(SEM[f"var{n}"], 1)
                pool.wait_ge(*count(f"var{n}", g, k + 1))
                pool.tensor_tensor(rstd[layer][:, lo:hi], var[layer][:, lo:hi], negh[:, lo:hi],
                                   ALU.pow).then_inc(SEM[f"rstd{n}"], 1)

            def graph_a(g, i):
                pool.wait_ge(*count("rdeg_ready", g, 1))
                pool.wait_ge(*count("adjB_in", g, 32))
                pool.wait_ge(*filled("meanT", 0, g, 1))
                pool.tensor_tensor(meanA[:, :, :], adjB[:, :, :],
                                   rdeg[:, :].rearrange("p (t a) -> p t a", a=1).broadcast_to([P, T, P]),
                                   ALU.mult).then_inc(SEM["meanA_ready"], 1)

            def graph_b(g, i):
                pool.wait_ge(*count("be_ready", g, 1))
                pool.wait_ge(*count("ht_ready", g, 1))
                pool.tensor_tensor(bhT[:, :, :], hT0[:, :, :],
                                   be[:, :].rearrange("p (t a) -> p t a", a=1).broadcast_to([P, T, P]),
                                   ALU.mult).then_inc(SEM["bht_ready"], 1)

            def gate_argument(g, i):
                pool.wait_ge(*filled("turn_h", HC - 1, g))
                pool.tensor_tensor(gate[:, :, :], wd[:, :].rearrange("p (a d) -> p a d", a=1).broadcast_to([P, T, D]),
                                   deg[:, :].rearrange("p (t a) -> p t a", a=1).broadcast_to([P, T, D]),
                                   ALU.mult).then_inc(SEM["z_ready"], 1)
                pool.wait_ge(*count("z_ready", g, 1))
                pool.tensor_tensor(gate[:, :, :], gate[:, :, :],
                                   bd[:, :].rearrange("p (a d) -> p a d", a=1).broadcast_to([P, T, D]),
                                   ALU.add).then_inc(SEM["z_ready"], 1)

            def split_low(g, i):
                for c in range(C):
                    pool.wait_ge(*count("xT_hi", g, c + 1))
                    pool.tensor_tensor(xT[1][:, c, :], xTin[:, c, :], xT[0][:, c, :].bitcast(F32),
                                       ALU.subtract).then_inc(SEM["xT_lo"], 1)

            def soft(g, k):
                u = unit(k)
                pool.wait_ge(*count("rsum_ready", g, k + 1))
                pool.tensor_tensor(rows_of(u), rows_of(u), srec[:, k, :].rearrange("p (h a) -> p h a", a=1)
                                   .broadcast_to([P, 2 * HP, N]), ALU.mult).then_inc(SEM["prob_ready"], 1)
                pool.wait_ge(*count("prob_ready", g, k + 1))
                pool.wait_ge(*count("mix_ready", g, 1))
                t = k - k % 2
                pool.tensor_tensor(u, u, mix[:, t:t + 2, :].rearrange("p t (a n) -> p t a n", a=1)
                                   .broadcast_to([P, 2, HP, N]), ALU.add).then_inc(SEM["attn_ready"], 1)

            steps = {
                "soft": soft, "mask": residual, "pv": biases, "graph_a": graph_a, "graph_b": graph_b, "gate": gate_argument, "split_low": split_low,
                "out0": lambda g, i: inv_root(g, 0, "0", 2 * i, 2 * i + 2, i),
                "mean": lambda g, i: inv_root(g, 1, "1", 2 * i, 2 * i + 2, i),
                "hyper": lambda g, i: inv_root(g, 2, "2", 2 * i, 2 * i + 2, i),
                "out3": lambda g, i: inv_root(g, 3, "3", 2 * i, 2 * i + 2, i),
                "up": lambda g, i: inv_root(g, 4, "_h", i, i + 1, i),
            }
            rounds(pool, lambda n, a, b, c: run(steps, n, a, b, c))

        @block.scalar
        def _(act):
            def row(ap, n=P):
                return ap.rearrange("(a n) -> a n", a=1).broadcast_to([n, ap.shape[0]])

            act.dma_start(gam[:, :], gamma_c).then_inc(bias_in, 16)
            act.dma_start(bet[:, :], beta_c).then_inc(bias_in, 16)
            act.dma_start(b1row, row(b1, 1)).then_inc(bias_in, 16)
            act.dma_start(b2row[:, 0:D], row(b2, 1)).then_inc(bias_in, 16)
            act.dma_start(b2row[:, D:2 * D], row(bl, 1)).then_inc(bias_in, 16)
            act.dma_start(bout[:, :], row(b_out)).then_inc(bias_in, 16)
            act.dma_start(wd[:, :], row(wd_r)).then_inc(bias_in, 16)
            act.dma_start(bd[:, :], row(bd_r)).then_inc(bias_in, 16)

            def split(g, i):
                for c in range(C):
                    act.wait_ge(*count("xT_in", g, 32))
                    act.wait_ge(*filled("v", T - 1, g, 1))
                    act.activation(xT[0][:, c, :], xTin[:, c, :], ACT.Copy).then_inc(SEM["xT_hi"], 1)

            def copy_out(g, fill, i, dst, ready, func=ACT.Copy, **kw):
                act.wait_ge(*filled(fill, i, g))
                src = bank_of(fill, i)
                act.activation(dst, src[:, :], func, **kw).then_inc(SEM[ready], 1)

            def mixmat(g, i):
                act.wait_ge(*count("adjA_in", g, 16))
                act.activation(expA[:, :, :], adjA[:, :, :], ACT.Exp, scale=-1.0).then_inc(SEM["expA_ready"], 1)

            def val(g, i):
                act.wait_ge(*filled("v", i, g))
                src = bank_of("v", i)[:, :].rearrange("n (p e d) -> n e p d", e=2, d=DH)
                for gr in range(2):
                    for e in range(2):
                        ins = act.activation(v[e * N:(e + 1) * N, i, gr, :, :], src[gr * N:(gr + 1) * N, e], ACT.Copy)
                ins.then_inc(SEM["v_ready"], 1)

            def shift(g, k):
                act.wait_ge(*count("shift_ready", g, k + 1))
                act.activation(rows_of(unit(k)), rows_of(unit(k)), ACT.Exp,
                               scale=float(DH) ** -0.5).then_inc(SEM["exp_ready"], 1)

            def pv(g, i):
                act.wait_ge(*filled("oT", i, g))
                src = bank_of("oT", i)
                ins = act.activation(oT[0][:, :, (i % 2) * P:(i % 2 + 1) * P],
                                     src[:, :].rearrange("p (a n) -> p a n", a=HP), ACT.Copy)
                ins.then_inc(SEM["oT_hi"], 1)

            def graph_a(g, i):
                act.wait_ge(*filled("ht", 0, g))
                src = bank_of("ht", 0)
                ins = act.activation(flat(hT0[:, :, :]), src[:, 0:T * P // 2].bitcast(BF16), ACT.Copy)
                ins.then_inc(SEM["ht_ready"], 1)

            def up(g, i):
                copy_out(g, "up", i, r[:, i, :], "relu_ready", ACT.Relu)

            def down(g, i):
                copy_out(g, "down", i, flat(yw[:, 2 * i:2 * i + 2, :]), "down_ready")

            def hyper(g, i):
                act.wait_ge(*count("z_ready", g, 2))
                act.activation(gate[:, 2 * i:2 * i + 2, :], gate[:, 2 * i:2 * i + 2, :], ACT.Tanh,
                               scale=0.5).then_inc(SEM["gate_ready"], 1)

            def qk(g, i):
                copy_out(g, "qk", i, qkT[:, i, :], "qk_tanh", ACT.Tanh, scale=0.25, bias=bqk[:, i:i + 1])

            steps = {
                "split": split, "mixmat": mixmat, "v": val, "shift": shift, "pv": pv, "graph_a": graph_a, "up": up,
                "down": down, "hyper": hyper, "qk": qk,
                "q": lambda g, i: copy_out(g, "q", i, qT[:, i, :], "q_ready"),
                "k": lambda g, i: copy_out(g, "k", i, kT[:, i, :], "k_ready"),
                "turnp": lambda g, i: copy_out(g, "pT", i, pT[:, i % 2].rearrange("p a n -> p (a n)"), "pT_ready"),
                "turn1": lambda g, i: copy_out(g, "turn1", i, x1T[0][:, i, :], "turn1_hi"),
                "agg": lambda g, i: copy_out(g, "agg", i, aggT[0][:, i, :], "agg_hi"),
                "graph_m": lambda g, i: copy_out(g, "meanT", 0, flat(meanT[:, :, :]), "meanT_ready"),
                "graph_d": lambda g, i: copy_out(g, "gT", 0, flat(gT[:, :, :]), "gT_ready"),
                "spread": lambda g, i: copy_out(g, "spread", i, spT[0][:, i, :], "spread_hi"),
                "turn_h": lambda g, i: copy_out(g, "turn_h", i, hT[0][:, i, :], "hT_hi"),
                "turn3": lambda g, i: copy_out(g, "turn3", i, xgT[0][:, i, :], "turn3_hi"),
                "turn_s": lambda g, i: copy_out(g, "turn_s", 0, flat(sT[:, :, :]), "sT_ready"),
                "agg3": lambda g, i: copy_out(g, "agg3", i, agg3[0][:, i, :], "agg3_hi"),
            }
            rounds(act, lambda n, a, b, c: run(steps, n, a, b, c))

        @block.vector
        def _(dve):
            done = [0]

            def setup(ins):
                done[0] += 1
                ins.then_inc(setup_dve, 1)
                dve.wait_ge(setup_dve, done[0])

            dve.wait_ge(early_in, 16 * 3)
            dve.tensor_copy(identb[:, :], ident[:, :]).then_inc(setup_dve, 1)
            dve.tensor_copy(ones3[:, :], onesf[:, :]).then_inc(setup_dve, 1)
            done[0] = 2

            def split_weight(pair, src):
                setup(dve.tensor_copy(pair[0][:, :, :], src))
                dve.tensor_tensor(pair[1][:, :, :], src, pair[0][:, :, :].bitcast(F32),
                                  ALU.subtract).then_inc(weights_ready, 1)

            for k, (pair, src) in enumerate(((wq, raw_q), (wk, raw_k), (wv, raw_v))):
                dve.wait_ge(qkv_in[k], 16 * C)
                split_weight(pair, src)

            def wide(ap, n):
                return ap.rearrange("p (t a) -> p t a", a=1).broadcast_to([ap.shape[0], ap.shape[1], n])

            def low_part(g, fill, i, lo, hi, name):
                dve.wait_ge(*count(f"{name}_hi", g, i + 1))
                src = bank_of(fill, i)[:, :]
                if len(lo.shape) == 3:
                    src = src.rearrange("p (a n) -> p a n", a=lo.shape[1])
                dve.tensor_tensor(lo, src, hi.bitcast(F32), ALU.subtract).then_inc(SEM[f"{name}_lo"], 1)

            def low_chunk(pair, fill, name):
                return lambda g, i: low_part(g, fill, i, pair[1][:, i, :], pair[0][:, i, :], name)

            def other_weights(i):
                if i == 0:
                    dve.wait_ge(weights_in, 16 * 9)
                    setup(dve.tensor_scalar(raw_o, raw_o, MIX, None, ALU.mult))
                    split_weight(wo, raw_o)
                    split_weight(w1, raw_1)
                if i == 1:
                    split_weight(wm, raw_m)
                    split_weight(wqk, raw_qk)
                if i == 2:
                    setup(dve.tensor_scalar(raw_lr, raw_lr, 0.5, None, ALU.mult))
                    setup(dve.tensor_scalar(bqk[:, :], bqk[:, :], 0.5, None, ALU.mult))
                    split_weight(wlr, raw_lr)
                if i == 3:
                    dve.wait_ge(bias_in, 16 * 8)
                    dve.wait_ge(t_full, 1)
                    dve.tensor_copy(trow, bank[7][0:1, 0:D]).then_inc(t_ready, 1)
                    for c in range(HC):
                        ins = dve.tensor_scalar(raw_2[:, c, :], raw_2[:, c, :], gam[:, c:c + 1], None, ALU.mult)
                    setup(ins)
                    split_weight(w2, raw_2)

            def pv(g, i):
                if isinstance(g, int) and g == 0:
                    other_weights(i)
                at = slice((i % 2) * P, (i % 2 + 1) * P)
                low_part(g, "oT", i, oT[1][:, :, at], oT[0][:, :, at], "oT")

            def norm(g, layer, src, lo, hi):
                n = "_h" if layer == 4 else str(layer)
                for t in range(lo, hi):
                    dve.bn_stats(stats[layer][:, t, :], src[:, t, :]).then_inc(SEM[f"stats{n}"], 1)
                for t in range(lo, hi):
                    dve.wait_ge(*count(f"stats{n}", g, t + 1))
                    apart(dve, g)
                    dve.bn_aggr(mv[layer][:, t, :], stats[layer][:, t, :]).then_inc(SEM[f"mv{n}"], 1)

            def scale(g, layer, x, lo, hi, ready, k):
                n = "_h" if layer == 4 else str(layer)
                dve.wait_ge(*count(f"rstd{n}", g, k + 1))
                for t in range(lo, hi):
                    ins = dve.tensor_scalar(x[:, t, :], x[:, t, :], mv[layer][:, t, 0:1],
                                            rstd[layer][:, t:t + 1], ALU.subtract, ALU.mult)
                ins.then_inc(SEM[ready], 1)

            def mask(g, i):
                dve.wait_ge(*count("mask_in", g, 16))
                dve.scalar_tensor_tensor(out=mi[:, :, :], in0=masks[:, 0:T * P].rearrange("p (t n) -> p t n", n=P),
                                         scalar=mcst[:, 0:1], in1=mcst[:, 1:1 + P].rearrange("p (a n) -> p a n", a=1)
                                         .broadcast_to([4, T, P]), op0=ALU.max, op1=ALU.mult)\
                   .then_inc(SEM["mask_rows"], 1)
                dve.tensor_scalar(flat(mj[:, :, :]), masks[:, T * P:T * (P + N)], mcst[:, 0:1], None,
                                  ALU.max).then_inc(SEM["mask_rows"], 1)

            def mixmat(g, i):
                dve.wait_ge(*filled("mixmat", 0, g))
                src = bank_of("mixmat", 0)
                ins = dve.tensor_scalar(flat(mm01[:, :, :]), src[:, 0:T * N], 1.0 / BIG, 1.0, ALU.mult, ALU.add)
                ins.then_inc(SEM["mm_ready"], 1)
                dve.wait_ge(*count("expA_ready", g, 1))
                dve.wait_ge(*count("adjA_in", g, 16))
                dve.tensor_tensor(mix[:, :, :], expA[:, :, :], adjA[:, :, :], ALU.add).then_inc(SEM["mix_sum"], 1)
                dve.wait_ge(*count("mm_ready", g, 1))
                dve.wait_ge(*count("mix_sum", g, 1))
                dve.tensor_tensor(mix[:, :, :], mix[:, :, :], mm01[:, :, :], ALU.mult).then_inc(SEM["mix_ready"], 1)

            def shift(g, k):
                fill = "s_odd" if k % 2 else "s_even"
                dve.wait_ge(*filled(fill, k // 2, g))
                src = bank_of(fill, k // 2)[:, :].rearrange("p (h n) -> p h n", n=N)
                dve.tensor_reduce(smax[:, k, :], src, AX.X, ALU.max).then_inc(SEM["max_ready"], 1)
                dve.wait_ge(*count("max_ready", g, k + 1))
                dve.tensor_tensor(rows_of(unit(k)), src, wide(smax[:, k, :], N),
                                  ALU.subtract).then_inc(SEM["shift_ready"], 1)

            def soft(g, k):
                dve.wait_ge(*count("exp_ready", g, k + 1))
                dve.tensor_reduce(ssum[:, k, :], rows_of(unit(k)), AX.X, ALU.add).then_inc(SEM["sum_ready"], 1)
                dve.wait_ge(*count("sum_ready", g, k + 1))
                dve.reciprocal(srec[:, k, :], ssum[:, k, :]).then_inc(SEM["rsum_ready"], 1)

            def out0(g, i):
                lo, hi = 2 * i, 2 * i + 2
                dve.wait_ge(*filled("out0", i, g))
                src = bank_of("out0", i)
                dve.wait_ge(*count("xb_ready", g, 1))
                ins = dve.tensor_tensor(flat(xl[0][:, lo:hi, :]), src[:, :], flat(xin[:, lo:hi, :]), ALU.add)
                ins.then_inc(SEM["sum0_ready"], 1)
                dve.wait_ge(*count("sum0_ready", g, i + 1))
                norm(g, 0, xl[0], lo, hi)

            def graph_a(g, i):
                dve.wait_ge(*count("adjB_in", g, 32))
                dve.tensor_scalar(edge[:, :, :], adjB[:, :, :], 0.0, None, ALU.not_equal).then_inc(SEM["edge_ready"], 1)
                dve.tensor_reduce(deg[:, :], adjB[:, :, :], AX.X, ALU.add).then_inc(SEM["deg_ready"], 1)
                dve.wait_ge(*count("deg_ready", g, 1))
                dve.tensor_scalar(degm[:, :], deg[:, :], 1e-6, None, ALU.max).then_inc(SEM["degmax"], 1)
                dve.wait_ge(*count("degmax", g, 1))
                dve.reciprocal(rdeg[:, :], degm[:, :]).then_inc(SEM["rdeg_ready"], 1)

            def graph_b(g, i):
                dve.wait_ge(*filled("cnt", 0, g))
                src = bank_of("cnt", 0)
                dve.tensor_scalar(cntm[:, :], src[:, 0:T], 1.0, None, ALU.max).then_inc(SEM["cntmax"], 1)
                dve.tensor_scalar(dpos[:, :], src[:, 2 * T:3 * T], 0.0, None, ALU.is_gt).then_inc(SEM["dsign"], 1)
                dve.tensor_scalar(dneg[:, :], src[:, 2 * T:3 * T], 0.0, None, ALU.is_le).then_inc(SEM["dsign"], 1)
                dve.wait_ge(*count("cntmax", g, 1))
                dve.reciprocal(be[:, :], cntm[:, :]).then_inc(SEM["be_ready"], 1)
                dve.wait_ge(*count("dsign", g, 2))
                ins = dve.scalar_tensor_tensor(out=dsafe[:, :], in0=src[:, 2 * T:3 * T], scalar=0.0, in1=dneg[:, :],
                                               op0=ALU.max, op1=ALU.add)
                ins.then_inc(SEM["dsafe"], 1)
                dve.wait_ge(*count("dsafe", g, 1))
                dve.reciprocal(drec[:, :], dsafe[:, :]).then_inc(SEM["drec"], 1)
                dve.wait_ge(*count("drec", g, 1))
                dve.tensor_tensor(dn[:, :], drec[:, :], dpos[:, :], ALU.mult).then_inc(SEM["dn_ready"], 1)

            def graph_c(g, i):
                dve.wait_ge(*filled("sym", 0, g))
                src = bank_of("sym", 0)
                dve.wait_ge(*count("dn_ready", g, 1))
                ins = dve.tensor_tensor(gmat[:, :, :], src[:, :].rearrange("p (t n) -> p t n", t=T),
                                        wide(dn[:, :], P), ALU.mult)
                ins.then_inc(SEM["g_ready"], 1)

            def mean(g, i):
                lo, hi = 2 * i, 2 * i + 2
                dve.wait_ge(*filled("mean", i, g))
                src = bank_of("mean", i)
                dve.wait_ge(*count("x1_ready", g, 2))
                dve.wait_ge(*count("out_done", g, 32, 1))
                ins = dve.scalar_tensor_tensor(out=flat(xl[1][:, lo:hi, :]), in0=src[:, :], scalar=0.0,
                                               in1=flat(xl[0][:, lo:hi, :]), op0=ALU.max, op1=ALU.add)
                ins.then_inc(SEM["sum1_ready"], 1)
                dve.wait_ge(*count("sum1_ready", g, i + 1))
                norm(g, 1, xl[1], lo, hi)

            def up(g, i):
                dve.wait_ge(*count("relu_ready", g, i + 1))
                norm(g, 4, r, i, i + 1)
                if i > 0:
                    scale(g, 4, r, i - 1, i, "h_ready", i - 1)
                if i == T - 1:
                    scale(g, 4, r, i, i + 1, "h_ready", i)

            def qk(g, i):
                dve.wait_ge(*count("qk_tanh", g, i + 1))
                dve.tensor_scalar(qkT[:, i, :], qkT[:, i, :], 1.0, None, ALU.add).then_inc(SEM["qk_ready"], 1)

            def hyper(g, i):
                lo, hi = 2 * i, 2 * i + 2
                dve.wait_ge(*filled("hyper", i, g))
                src = bank_of("hyper", i)
                dve.wait_ge(*count("x2_ready", g, 2))
                ins = dve.scalar_tensor_tensor(out=flat(xl[2][:, lo:hi, :]), in0=flat(xl[1][:, lo:hi, :]), scalar=2.0,
                                               in1=src[:, :], op0=ALU.mult, op1=ALU.add)
                ins.then_inc(SEM["sum2_ready"], 1)
                dve.wait_ge(*count("sum2_ready", g, i + 1))
                norm(g, 2, xl[2], lo, hi)

            def gated(g, k):
                scale(g, 2, xl[2], 2 * k, 2 * k + 2, "x3_ready", k)
                dve.wait_ge(*count("x3_ready", g, k + 1))
                dve.wait_ge(*count("gate_ready", g, k + 1))
                dve.scalar_tensor_tensor(out=flat(xg[:, 2 * k:2 * k + 2, :]),
                                         in0=flat(gate[:, 2 * k:2 * k + 2, :]), scalar=1.0,
                                         in1=flat(xl[2][:, 2 * k:2 * k + 2, :]),
                                         op0=ALU.add, op1=ALU.mult).then_inc(SEM["xg_ready"], 1)

            def simi(g, i):
                dve.wait_ge(*filled("sim", 0, g))
                src = bank_of("sim", 0)
                dve.wait_ge(*count("adjB_in", g, 32))
                ins = dve.tensor_tensor(flat(sim[:, :, :]), src[:, :], flat(adjB[:, :, :]), ALU.mult)
                ins.then_inc(SEM["sim_ready"], 1)
                dve.wait_ge(*count("sim_ready", g, 1))
                dve.tensor_reduce(simsum[:, :], sim[:, :, :], AX.X, ALU.add).then_inc(SEM["simsum"], 1)
                dve.wait_ge(*count("simsum", g, 1))
                dve.tensor_scalar(simeps[:, :], simsum[:, :], 64e-6, None, ALU.add).then_inc(SEM["simeps"], 1)
                dve.wait_ge(*count("simeps", g, 1))
                dve.reciprocal(simrec[:, :], simeps[:, :]).then_inc(SEM["simrec"], 1)
                dve.wait_ge(*count("simrec", g, 1))
                dve.tensor_tensor(smat[:, :, :], sim[:, :, :], wide(simrec[:, :], P), ALU.mult).then_inc(SEM["s_ready"], 1)

            def out3(g, i):
                lo, hi = 2 * i, 2 * i + 2
                dve.wait_ge(*filled("out3", i, g))
                src = bank_of("out3", i)
                ins = dve.scalar_tensor_tensor(out=flat(xl[3][:, lo:hi, :]), in0=src[:, :], scalar=0.0,
                                               in1=flat(xl[2][:, lo:hi, :]), op0=ALU.max, op1=ALU.add)
                ins.then_inc(SEM["sum3_ready"], 1)
                dve.wait_ge(*count("sum3_ready", g, i + 1))
                norm(g, 3, xl[3], lo, hi)

            steps = {
                "mask": mask, "mixmat": mixmat, "shift": shift, "soft": soft, "pv": pv, "out0": out0,
                "graph_a": graph_a, "graph_b": graph_b, "graph_c": graph_c, "mean": mean, "up": up, "hyper": hyper,
                "qk": qk, "sim": simi, "out3": out3, "gated": gated,
                "scale0": lambda g, i: scale(g, 0, xl[0], 2 * i, 2 * i + 2, "x1_ready", i),
                "scale1": lambda g, i: [scale(g, 1, xl[1], 2 * k, 2 * k + 2, "x2_ready", k) for k in range(2)],
                "scale3": lambda g, i: [scale(g, 3, xl[3], 2 * k, 2 * k + 2, "x4_ready", k) for k in range(2)],
                "turn1": low_chunk(x1T, "turn1", "turn1"), "agg": low_chunk(aggT, "agg", "agg"),
                "spread": low_chunk(spT, "spread", "spread"), "turn_h": low_chunk(hT, "turn_h", "hT"),
                "turn3": low_chunk(xgT, "turn3", "turn3"), "agg3": low_chunk(agg3, "agg3", "agg3"),
            }
            rounds(dve, lambda n, a, b, c: run(steps, n, a, b, c))

        @block.tensor
        def _(pe):
            pe.wait_ge(setup_dve, 2)

            def product(out_ap, pairs, bias=None):
                if bias is not None:
                    pe.matmul(out_ap, ones3[0:96, :], bias3[:, bias[0]:bias[1]], start=True, stop=False)
                for j, (l, rr) in enumerate(pairs):
                    pe.matmul(out_ap, l[0], rr[0], start=(bias is None and j == 0), stop=False)
                    pe.matmul(out_ap, l[0], rr[1], start=False, stop=False)
                    ins = pe.matmul(out_ap, l[1], rr[0], start=False, stop=(j == len(pairs) - 1))
                return ins

            def tile_of(pair, c, t):
                return [x[:, c, t * P:(t + 1) * P] for x in pair]

            def chunk(pair, c, cols=slice(None)):
                return [x[:, c, cols] for x in pair]

            def mixmat(g, i):
                pe.wait_ge(*count("mask_rows", g, 2))
                pe.wait_ge(*emptied("mixmat", 0, g))
                dst = bank_of("mixmat", 0)
                apart(pe, g)
                for t in range(T):
                    ins = pe.matmul(dst[:, t * N:(t + 1) * N], mi[:, t, :], mj[:, t, :],
                                    start=True, stop=True)
                now_full(ins, "mixmat", 0)

            def beta_row():
                pe.wait_ge(weights_in, 16 * 9)
                pe.wait_ge(bias_in, 16 * 8)
                for c in range(HC):
                    ins = pe.matmul(bank[7][0:1, 0:D], bet[:, c:c + 1], raw_2[:, c, :], start=(c == 0),
                                    stop=(c == HC - 1))
                ins.then_inc(t_full, 1)

            def proj(name, w, g, i):
                if isinstance(g, int) and g == 0 and i == 0:
                    pe.wait_ge(weights_ready, 1 if name == "q" else 2)
                pe.wait_ge(*count("xT_lo", g, 2))
                pe.wait_ge(*emptied(name, i, g))
                dst = bank_of(name, i)
                now_full(product(dst[:, :], [(chunk(w, c, slice(i * P, (i + 1) * P)), chunk(xT, c)) for c in range(C)]), name, i)

            def val(g, i):
                if isinstance(g, int) and g == 0 and i == 0:
                    pe.wait_ge(weights_ready, 3)
                pe.wait_ge(*emptied("v", i, g))
                dst = bank_of("v", i)
                now_full(product(dst[:, :], [(tile_of(xT, c, i), chunk(wv, c)) for c in range(C)]), "v", i)

            def score(g, i):
                pe.wait_ge(*count("q_ready", g, HP))
                pe.wait_ge(*count("k_ready", g, HP))
                pe.wait_ge(*emptied("s_odd", i, g))
                dst = [bank_of("s_even", i), bank_of("s_odd", i)]
                apart(pe, g)
                for e in range(2):
                    for k in range(2):
                        pe.matmul(dst[e][:, k * HP * N:(k + 1) * HP * N], mi[:, 2 * i + k, :],
                                  mj[:, 2 * i + k:2 * i + k + 1, :].broadcast_to([4, HP, N]),
                                  start=(k == 0), stop=False, skip_group_check=True)
                ins = None
                for k in range(2):
                    for p in range(HP):
                        for gr in range(2):
                            for e in range(2):
                                tok = slice((2 * i + k) * P + gr * N, (2 * i + k) * P + (gr + 1) * N)
                                col = (k * HP + p) * N
                                ins0, ins = ins, pe.matmul(dst[e][gr * N:(gr + 1) * N, col:col + N],
                                                qT[e * DH:(e + 1) * DH, p, tok], kT[e * DH:(e + 1) * DH, p, tok],
                                                start=False, stop=(k == 1 and p == HP - 1), skip_group_check=True)
                now_full(ins0, "s_even", i)
                now_full(ins, "s_odd", i)

            def turnp(g, i):
                pe.wait_ge(*count("attn_ready", g, i - i % 2 + 2))
                pe.wait_ge(*emptied("pT", i, g))
                dst = bank_of("pT", i)
                for p in range(HP):
                    ins = pe.transpose(dst[:, p * P:(p + 1) * P],
                                       prob[:, i, p].rearrange("p e n -> p (e n)"), ident[:, :])
                now_full(ins, "pT", i)

            def pv(g, i):
                pe.wait_ge(*count("pT_ready", g, i + 1))
                pe.wait_ge(*count("v_ready", g, i + 1))
                pe.wait_ge(*emptied("oT", i, g))
                dst = bank_of("oT", i)
                apart(pe, g)
                for p in range(HP):
                    for gr in range(2):
                        for e in range(2):
                            rows = slice(e * N, (e + 1) * N)
                            ins = pe.matmul(dst[rows, p * P + gr * N:p * P + (gr + 1) * N], v[rows, i, gr, p, :],
                                            pT[rows, i % 2, p, gr * N:(gr + 1) * N], start=True, stop=True,
                                            skip_group_check=True)
                now_full(ins, "oT", i)

            def two_tiles(name, i, pairs_of, bias=None):
                dst = bank_of(name, i)
                for k in range(2):
                    ins = product(dst[:, k * D:(k + 1) * D], pairs_of(2 * i + k), bias)
                now_full(ins, name, i)

            def out0(g, i):
                if isinstance(g, int) and g == 0 and i == 0:
                    beta_row()
                    pe.wait_ge(weights_ready, 4)
                pe.wait_ge(*count("oT_lo", g, 2 * i + 2))
                pe.wait_ge(*emptied("out0", i, g))
                two_tiles("out0", i, lambda t: [(tile_of(oT, p, t % 2), chunk(wo, p)) for p in range(HP)])

            def turned(name, g, i, src, ready, n):
                pe.wait_ge(*count(ready, g, n))
                pe.wait_ge(*emptied(name, i, g))
                dst = bank_of(name, i)
                for t in range(T):
                    ins = pe.transpose(dst[:, t * P:(t + 1) * P], src[:, t, i * P:(i + 1) * P], ident[:, :])
                now_full(ins, name, i)

            def graph_a(g, i):
                pe.wait_ge(*count("edge_ready", g, 1))
                pe.wait_ge(*emptied("ht", 0, g))
                dst = bank_of("ht", 0)[:, 0:T * P // 2].bitcast(BF16)
                for t in range(T):
                    ins = pe.transpose(dst[:, t * P:(t + 1) * P], edge[:, t, :], identb[:, :])
                now_full(ins, "ht", 0)

            def graph_b(g, i):
                pe.wait_ge(*count("ht_ready", g, 1))
                pe.wait_ge(*emptied("cnt", 0, g))
                dst = bank_of("cnt", 0)
                for t in range(T):
                    pe.matmul(dst[:, t:t + 1], edge[:, t, :], onescol[:, 0:1], start=True, stop=True)
                for t in range(T):
                    ins = pe.matmul(dst[:, 2 * T + t:2 * T + t + 1], hT0[:, t, :],
                                    row0[:, bass.ds(g * T + t, 1)], start=True, stop=True)
                now_full(ins, "cnt", 0)

            def graph_c(g, i):
                pe.wait_ge(*count("bht_ready", g, 1))
                pe.wait_ge(*emptied("sym", 0, g))
                dst = bank_of("sym", 0)
                for t in range(T):
                    ins = pe.matmul(dst[:, t * P:(t + 1) * P], hT0[:, t, :], bhT[:, t, :], start=True, stop=True)
                now_full(ins, "sym", 0)

            def graph_m(g, i):
                pe.wait_ge(*count("meanA_ready", g, 1))
                pe.wait_ge(*emptied("meanT", 0, g))
                dst = bank_of("meanT", 0)
                for t in range(T):
                    ins = pe.transpose(dst[:, t * P:(t + 1) * P], meanA[:, t, :], ident[:, :])
                now_full(ins, "meanT", 0)

            def graph_d(g, i):
                pe.wait_ge(*count("g_ready", g, 1))
                pe.wait_ge(*emptied("gT", 0, g))
                dst = bank_of("gT", 0)
                for t in range(T):
                    ins = pe.transpose(dst[:, t * P:(t + 1) * P], gmat[:, t, :], ident[:, :])
                now_full(ins, "gT", 0)

            def gathered(name, g, i, src, mat):
                pe.wait_ge(*emptied(name, i, g))
                dst = bank_of(name, i)
                for t in range(T):
                    ins = pe.matmul(dst[:, t * P:(t + 1) * P], src[:, t, i * P:(i + 1) * P], mat[:, t, :],
                                    start=True, stop=True)
                now_full(ins, name, i)

            def agg(g, i):
                pe.wait_ge(*count("meanT_ready", g, 1))
                gathered("agg", g, i, xl[0], meanT)

            def mean(g, i):
                if isinstance(g, int) and g == 0 and i == 0:
                    pe.wait_ge(weights_ready, 9)
                    pe.wait_ge(bias_ready, 18)
                pe.wait_ge(*count("turn1_lo", g, 2))
                pe.wait_ge(*count("agg_lo", g, 2))
                two_tiles("mean", i, lambda t: [(tile_of(x1T, c, t), chunk(wm, c)) for c in range(C)]
                          + [(tile_of(aggT, c, t), chunk(wm, C + c)) for c in range(C)])

            def spread(g, i):
                pe.wait_ge(*count("x2_ready", g, 2))
                pe.wait_ge(*count("gT_ready", g, 1))
                gathered("spread", g, i, xl[1], gT)

            def up(g, i):
                pe.wait_ge(*count("spread_lo", g, 2))
                pe.wait_ge(*emptied("up", i, g))
                dst = bank_of("up", i)
                now_full(product(dst[:, :], [(tile_of(spT, c, i), chunk(w1, c)) for c in range(C)], (0, HID)), "up", i)

            def down(g, i):
                pe.wait_ge(*count("hT_lo", g, HC))
                pe.wait_ge(*emptied("down", i, g))
                two_tiles("down", i, lambda t: [(tile_of(hT, c, t), chunk(w2, c)) for c in range(HC)],
                          (HID + 2 * D, NBIAS))

            def hyper(g, i):
                pe.wait_ge(*count("down_ready", g, i + 1))
                pe.wait_ge(*emptied("hyper", i, g))
                dst = bank_of("hyper", i)
                for k in range(2):
                    half = dst[:, k * D:(k + 1) * D]
                    pe.matmul(half, ones3[0:96, :], bias3[:, HID:HID + D], start=True, stop=False)
                    ins = pe.matmul(half, gT[:, 2 * i + k, :], yw[:, 2 * i + k, :], start=False, stop=True)
                now_full(ins, "hyper", i)

            def qk(g, i):
                pe.wait_ge(*count("turn3_lo", g, 2))
                pe.wait_ge(*emptied("qk", i, g))
                dst = bank_of("qk", i)
                now_full(product(dst[:, :], [(chunk(wqk, c, slice(i * P, (i + 1) * P)), chunk(xgT, c)) for c in range(C)]), "qk", i)

            def simi(g, i):
                pe.wait_ge(*count("qk_ready", g, 2))
                pe.wait_ge(*emptied("sim", 0, g))
                dst = bank_of("sim", 0)
                for t in range(T):
                    for c in range(C):
                        tile = qkT[:, c, t * P:(t + 1) * P]
                        ins = pe.matmul(dst[:, t * P:(t + 1) * P], tile, tile, start=(c == 0), stop=(c == C - 1))
                now_full(ins, "sim", 0)

            def turn_s(g, i):
                pe.wait_ge(*count("s_ready", g, 1))
                pe.wait_ge(*emptied("turn_s", 0, g))
                dst = bank_of("turn_s", 0)
                for t in range(T):
                    ins = pe.transpose(dst[:, t * P:(t + 1) * P], smat[:, t, :], ident[:, :])
                now_full(ins, "turn_s", 0)

            def agg3_(g, i):
                pe.wait_ge(*count("sT_ready", g, 1))
                gathered("agg3", g, i, xg, sT)

            def out3(g, i):
                pe.wait_ge(*count("agg3_lo", g, 2))
                pe.wait_ge(*emptied("out3", i, g))
                two_tiles("out3", i, lambda t: [(tile_of(agg3, c, t), chunk(wlr, c)) for c in range(C)]
                          + [(tile_of(xgT, c, t), chunk(wlr, C + c)) for c in range(C)], (HID + D, HID + 2 * D))

            steps = {
                "mixmat": mixmat, "q": lambda g, i: proj("q", wq, g, i), "k": lambda g, i: proj("k", wk, g, i),
                "v": val, "score": score, "turnp": turnp, "pv": pv, "out0": out0,
                "turn1": lambda g, i: turned("turn1", g, i, xl[0], "x1_ready", 2),
                "graph_a": graph_a, "graph_b": graph_b, "graph_m": graph_m, "graph_c": graph_c, "graph_d": graph_d, "agg": agg,
                "mean": mean, "spread": spread, "up": up,
                "turn_h": lambda g, i: turned("turn_h", g, i, r, "h_ready", T),
                "down": down, "hyper": hyper,
                "turn3": lambda g, i: turned("turn3", g, i, xg, "xg_ready", 2),
                "qk": qk, "sim": simi, "turn_s": turn_s, "agg3": agg3_, "out3": out3,
            }
            rounds(pe, lambda n, a, b, c: run(steps, n, a, b, c))


def kernel(**inputs):
    import numpy as _np
    import concourse.bacc as _bacc
    from concourse import mybir as _mybir
    from concourse.bass_utils import run_bass_kernel_spmd as _run

    a = {k: _np.asarray(v) for k, v in inputs.items()}
    ident = _np.eye(P, dtype=_np.float32)
    ones3 = _np.zeros((P, P), _np.float32)
    ones3[[0, 32, 64]] = 1.0
    mrow = _np.zeros((4, 1 + P), _np.float32)
    mrow[:, 0] = [1, 0, 1, 0]
    mrow[0:2, 1:1 + N] = [[-BIG], [BIG]]
    mrow[2:4, 1 + N:] = [[-BIG], [BIG]]
    m = a["nodemask"]
    rows = _np.broadcast_to(m.reshape(1, GRP, T * P), (4, GRP, T * P))
    cols = _np.repeat(_np.moveaxis(m.reshape(GRP, T, 2, N), 2, 0), 2, axis=0).reshape(4, GRP, T * N)
    arrays = {
        "x": a["x"], "x_t": a["x"].reshape(B * N, D).T, "adj": a["adj"],
        "adj_row0": a["adj"][:, 0, :].reshape(B // 2, P).T, "mask_rows": _np.concatenate([rows, cols], axis=2).reshape(4, -1),
        "wqkv": a["L0_gnn_W_qkv"], "w_out": a["L0_gnn_W_out"], "b_out": a["L0_gnn_b_out"],
        "w_mean_t": a["L1_gnn_W"].T, "w1_t": a["L2_gnn_W1"].T, "b1": a["L2_gnn_b1"],
        "gamma_c": a["L2_gnn_gamma"].reshape(HC, P).T, "beta_c": a["L2_gnn_beta"].reshape(HC, P).T,
        "w2_t": a["L2_gnn_W2"].T, "b2": a["L2_gnn_b2"], "wqk_t": a["L3_gnn_Wqk"].T,
        "bqk_c": a["L3_gnn_bqk"].reshape(C, P).T, "wl_t": a["L3_gnn_Wl"].T, "bl": a["L3_gnn_bl"],
        "wr_t": a["L3_gnn_Wr"].T, "wd_r": a["L3_gnn_Wd"].reshape(D), "bd_r": a["L3_gnn_bd"],
        "ident_c": ident, "ones3_c": ones3, "mrow_c": mrow,
    }
    nc = _bacc.Bacc("TRN2", target_bir_lowering=False, num_devices=1)
    maps, args = {}, []
    for name, arr in arrays.items():
        arr = _np.ascontiguousarray(arr)
        maps[f"in_{name}"] = arr
        args.append(nc.dram_tensor(f"in_{name}", arr.shape, _mybir.dt.from_np(arr.dtype), kind="ExternalInput").ap())
    out = nc.dram_tensor("out_x", (B, N, D), F32, kind="ExternalOutput").ap()
    graph_layers(nc, *args, out)
    r = _run(nc, [maps], core_ids=[0])
    return r.results[0]["out_x"]
```

```python
from contextlib import ExitStack

import concourse.bass as bass
from concourse import mybir

ALU = mybir.AluOpType
ACT = mybir.ActivationFunctionType
AX = mybir.AxisListType
F32 = mybir.dt.float32
F32R = mybir.dt.float32r
BF16 = mybir.dt.bfloat16
U8 = mybir.dt.uint8

P = 128
N = 64
D = 256
B = 128
H = 8
DH = 64
HID = 512
T = 4
GRP = B * N // (T * P)
TOK = T * P
C = D // P
HP = H // 2
HC = HID // P
NBIAS = HID + 3 * D
EPS_LN = 1e-5
MIX = 0.33
BIG = 2.0 ** 120

SCHEDULE = [
    ("B", "turn1", 0), ("B", "turn1", 1), ("A", "k", 1), ("B", "graph_a", 0), ("C", "scale3", 0), ("A", "k", 2),
    ("B", "graph_b", 0), ("B", "graph_m", 0), ("A", "mask", 0), ("A", "k", 3), ("B", "agg", 0), ("B", "agg", 1),
    ("B", "graph_c", 0), ("A", "mixmat", 0), ("A", "score", 0), ("A", "shift", 0), ("B", "graph_d", 0),
    ("A", "shift", 1), ("B", "mean", 0), ("B", "mean", 1), ("A", "v", 0), ("B", "scale1", 0), ("A", "v", 1),
    ("A", "v", 2), ("A", "soft", 0), ("A", "soft", 1), ("B", "spread", 0), ("B", "spread", 1), ("A", "v", 3),
    ("B", "up", 0), ("B", "up", 1), ("B", "up", 2), ("B", "up", 3), ("A", "score", 1),
    ("B", "turn_h", 0), ("B", "turn_h", 1), ("B", "turn_h", 2), ("B", "turn_h", 3), ("B", "gate", 0),
    ("A", "shift", 2), ("A", "shift", 3), ("N", "split", 0), ("A", "turnp", 0), ("A", "turnp", 1),
    ("B", "down", 0), ("A", "soft", 2), ("B", "down", 1), ("A", "soft", 3), ("A", "pv", 0), ("B", "hyper", 0),
    ("A", "pv", 1), ("B", "hyper", 1), ("N", "split_low", 0), ("B", "gated", 0), ("A", "turnp", 2), ("A", "turnp", 3),
    ("B", "gated", 1), ("A", "out0", 0), ("A", "pv", 2), ("B", "turn3", 0), ("B", "turn3", 1), ("A", "pv", 3),
    ("A", "norm0", 0), ("N", "q", 0), ("B", "qk", 0), ("B", "qk", 1), ("A", "scale0", 0), ("A", "out0", 1),
    ("B", "sim", 0), ("A", "norm0", 1), ("N", "q", 1), ("N", "q", 2), ("A", "scale0", 1), ("B", "turn_s", 0),
    ("N", "q", 3), ("B", "agg3", 0), ("B", "agg3", 1), ("N", "k", 0), ("B", "out3", 0), ("B", "out3", 1),
]

FILLS = {"graph_a": ["ht"], "graph_b": ["cnt"], "graph_c": ["sym"], "graph_m": ["meanT"], "graph_d": ["gT"],
         "score": ["s_even", "s_odd"], "turnp": ["pT"], "pv": ["oT"],
         "split": [], "split_low": [], "mask": [], "shift": [], "soft": [], "gate": [],
         "gated": [], "norm0": [], "scale0": [], "scale1": [], "scale3": []}
BANK = {}
PER_BANK = [0] * 8
_turn = {True: 0, False: 4}
_order = []
for _s, _n, _i in SCHEDULE:
    for _f in FILLS.get(_n, [_n]):
        _order.append((_turn[_s != "B"], _s == "N", _f, _i))
        _turn[_s != "B"] = (_turn[_s != "B"] + 1) % 4 + (4 if _s == "B" else 0)
for _k in range(8):
    _here = [x for x in _order if x[0] == _k]
    assert [x[1] for x in _here] == sorted(x[1] for x in _here)
    for _, _, _f, _i in sorted(_here, key=lambda x: not x[1]):
        BANK[(_f, _i)] = (_k, PER_BANK[_k])
        PER_BANK[_k] += 1

BEFORE = {}
for _key, (_b, _c) in BANK.items():
    _prev = (_c - 1) % PER_BANK[_b]
    BEFORE[_key] = (_b, next(k for k, v in BANK.items() if v == (_b, _prev)), 1 if _c == 0 else 0)
READ_OUT = {
    "mixmat": "mm_ready", "q": "q_ready", "k": "k_ready", "v": "v_ready", "pT": "pT_ready", "oT": "oT_lo",
    "out0": "sum0_ready", "turn1": "turn1_lo", "agg": "agg_lo", "mean": "sum1_ready", "ht": "ht_ready",
    "cnt": "dsum", "sym": "g_ready", "meanT": "meanT_ready", "gT": "gT_ready", "spread": "spread_lo",
    "up": "relu_ready", "turn_h": "hT_lo", "down": "down_ready", "hyper": "sum2_ready", "turn3": "turn3_lo",
    "qk": "qk_tanh", "sim": "sim_ready", "turn_s": "sT_ready", "agg3": "agg3_lo", "out3": "sum3_ready",
}


PER = {
    "xT_in": 32, "x_in": 16, "adjA_in": 16, "adjB_in": 32, "mask_in": 16, "out_done": 32,
    "xT_hi": 2, "xT_lo": 2, "mask_rows": 2,
    "residual_ready": 1, "expA_ready": 1, "mm_ready": 1, "mix_sum": 1, "mix_ready": 1,
    "q_ready": 4, "k_ready": 4, "v_ready": 4,
    "max_ready": 4, "shift_ready": 4, "exp_ready": 4, "sum_ready": 4, "rsum_ready": 4, "prob_ready": 4,
    "attn_ready": 4, "pT_ready": 4, "oT_hi": 4, "oT_lo": 4,
    "sum0_ready": 2, "stats0": 4, "mv0": 4, "var0": 2, "rstd0": 2, "x1_ready": 2,
    "turn1_hi": 2, "turn1_lo": 2, "agg_hi": 2, "agg_lo": 2,
    "edge_ready": 1, "deg_ready": 1, "degmax": 1, "rdeg_ready": 1, "meanA_ready": 1, "ht_ready": 1,
    "cntmax": 1, "be_ready": 1, "bht_ready": 1, "dsum": 1, "dsign": 2, "dsafe": 1, "drec": 1, "dn_ready": 1,
    "g_ready": 1, "meanT_ready": 1, "gT_ready": 1,
    "sum1_ready": 2, "stats1": 4, "mv1": 4, "var1": 2, "rstd1": 2, "x2_ready": 2,
    "spread_hi": 2, "spread_lo": 2, "relu_ready": 4, "stats_h": 4, "mv_h": 4, "var_h": 4, "rstd_h": 4, "h_ready": 4,
    "hT_hi": 4, "hT_lo": 4, "down_ready": 2,
    "sum2_ready": 2, "stats2": 4, "mv2": 4, "var2": 2, "rstd2": 2, "x3_ready": 2,
    "z_ready": 2, "gate_ready": 2, "xg_ready": 2, "turn3_hi": 2, "turn3_lo": 2, "qk_tanh": 2, "qk_ready": 2,
    "sim_ready": 1, "simsum": 1, "simeps": 1, "simrec": 1, "s_ready": 1, "sT_ready": 1, "agg3_hi": 2, "agg3_lo": 2,
    "sum3_ready": 2, "stats3": 4, "mv3": 4, "var3": 2, "rstd3": 2, "x4_ready": 2,
}


def graph_layers(nc, x, x_t, adj, adj_row0, mask_rows, wqkv, w_out, b_out, w_mean_t, w1_t, b1, gamma_c, beta_c, w2_t,
                 b2, wqk_t, bqk_c, wl_t, bl, wr_t, wd_r, bd_r, ident_c, ones3_c, mrow_c, out):
    with ExitStack() as ctx:
        def sb(name, shape, dt=F32):
            return ctx.enter_context(nc.sbuf_tensor(name, shape, dt))

        def split(name, shape):
            return [sb(name + "_hi", shape, F32R), sb(name + "_lo", shape, F32R)]

        def part(pair, *at):
            return [p[at] for p in pair]

        wq = split("wq", [P, C, H * DH])
        wk = split("wk", [P, C, H * DH])
        wv = split("wv", [P, C, H * DH])
        wo = split("wo", [P, HP, D])
        wm = split("wm", [P, 2 * C, D])
        w1 = split("w1", [P, C, HID])
        w2 = split("w2", [P, HC, D])
        wqk = split("wqk", [P, C, D])
        wlr = split("wlr", [P, 2 * C, D])
        ident = sb("ident", [P, P])
        identb = sb("identb", [P, P], BF16)
        ones3 = sb("ones3", [P, P], BF16)
        onescol = sb("onescol", [P, 2], BF16)
        bias3 = sb("bias3", [96, NBIAS], BF16)
        bout = sb("bout", [P, D])
        wd = sb("wd", [P, D])
        bd = sb("bd", [P, D])
        gam = sb("gam", [P, HC])
        bet = sb("bet", [P, HC])
        bqk = sb("bqk", [P, C])
        row0p = sb("row0p", [P, T * GRP, 3], BF16)
        negh = sb("negh", [P, T])
        warm = sb("warm", [P, T])
        mcst = sb("mcst", [4, 1 + P])
        masks = sb("masks", [4, T * (P + N)], U8)
        mi = sb("mi", [4, T, P], BF16)
        mj = sb("mj", [4, T, N], BF16)
        xTin = sb("xTin", [P, C, TOK])
        xT = split("xT", [P, C, TOK])
        xin = sb("xin", [P, T, D])
        adjA = sb("adjA", [P, T, N])
        expA = sb("expA", [P, T, N])
        mm01 = sb("mm01", [P, T, N])
        mix = sb("mix", [P, T, N])
        qT = sb("qT", [P, HP, TOK])
        kT = sb("kT", [P, HP, TOK])
        v = sb("v", [P, T, 2, HP, DH])
        prob = sb("prob", [P, T, HP, 2, N])
        smax = sb("smax", [P, T, 2 * HP])
        ssum = sb("ssum", [P, T, 2 * HP])
        srec = sb("srec", [P, T, 2 * HP])
        pT = sb("pT", [P, 2, HP, P])
        oT = split("oT", [P, HP, 2 * P])
        adjB = sb("adjB", [P, T, P])
        edge = sb("edge", [P, T, P], BF16)
        deg = sb("deg", [P, T])
        degm = sb("degm", [P, T])
        rdeg = sb("rdeg", [P, T])
        meanA = sb("meanA", [P, T, P])
        meanT = sb("meanT", [P, T, P])
        hT0 = sb("hT0", [P, T, P])
        bhT = sb("bhT", [P, T, P])
        hTb = sb("hTb", [P, T, P], BF16)
        cntm = sb("cntm", [P, T])
        dsum = sb("dsum", [P, T])
        be = sb("be", [P, T])
        dpos = sb("dpos", [P, T])
        dneg = sb("dneg", [P, T])
        dsafe = sb("dsafe", [P, T])
        drec = sb("drec", [P, T])
        dn = sb("dn", [P, T])
        gmat = sb("gmat", [P, T, P])
        gT = sb("gT", [P, T, P])
        hT = split("hT", [P, HC, TOK])
        x1T = part(hT, slice(None), slice(0, C))
        aggT = part(hT, slice(None), slice(C, 2 * C))
        agg3 = aggT
        spT = split("spT", [P, C, TOK])
        xgT = spT
        r = sb("r", [P, T, HID])
        qkT = r[:, 0:C, :]
        yw = sb("yw", [P, T, D])
        gate = r[:, C:2 * C, :].rearrange("p a (b d) -> p (a b) d", d=D)
        xg = yw
        sim = hT0
        smat = sim
        sT = bhT
        simsum = sb("simsum", [P, T])
        simeps = sb("simeps", [P, T])
        simrec = sb("simrec", [P, T])
        xl = [sb(f"x{i + 1}", [P, T, D]) for i in range(3)]
        xl.append(xl[1])
        stats = [sb(f"stats{i}", [P, T, 6]) for i in range(5)]
        mv = [sb(f"mv{i}", [P, T, 2]) for i in range(5)]
        var = [sb(f"var{i}", [P, T]) for i in range(5)]
        rstd = [sb(f"rstd{i}", [P, T]) for i in range(5)]

        def lent(ap, n, m):
            return ap.rearrange("p (c n) -> p c n", n=m)[:, 0:n, :]

        def flat(ap):
            return ap.rearrange("p t n -> p (t n)")

        raw_q, raw_k, raw_v = r[:, 0:2, :], r[:, 2:4, :], lent(flat(xl[1][:, :, :]), C, HID)
        raw_o, raw_m, raw_1 = xl[2][:, :, :], yw[:, :, :], lent(flat(xl[0][:, :, :]), C, HID)
        raw_2, raw_lr = lent(flat(raw_q), HC, D), lent(flat(raw_k), HC, D)
        raw_qk = lent(flat(hT0[:, :, :]), C, D)
        b1row, b2row = flat(bhT[0:1, :, :]), flat(meanA[0:1, :, :])
        trow = flat(meanT[0:1, :, :])[:, 0:D]
        onesf, row0 = meanT[:, 2, :], meanT[:, 3, 0:T * GRP]
        scratch_rows = [flat(gmat[0:1, :, :]), flat(gT[0:1, :, :])]

        bank = [ctx.enter_context(nc.psum_tensor(f"bank{i}", [P, 512], F32)) for i in range(8)]
        SEM = {n: ctx.enter_context(nc.semaphore(n)) for n in PER}
        full = [ctx.enter_context(nc.semaphore(f"bank{i}_full")) for i in range(8)]
        weights_in = ctx.enter_context(nc.semaphore("weights_in"))
        qkv_in = [ctx.enter_context(nc.semaphore(f"{n}_weights_in")) for n in "qkv"]
        wo_in = ctx.enter_context(nc.semaphore("wo_in"))
        bias_in = ctx.enter_context(nc.semaphore("bias_in"))
        t_full = ctx.enter_context(nc.semaphore("t_full"))
        weights_ready = ctx.enter_context(nc.semaphore("weights_ready"))
        early_in = ctx.enter_context(nc.semaphore("early_in"))
        zero_ready = ctx.enter_context(nc.semaphore("zero_ready"))
        parted = ctx.enter_context(nc.semaphore("parted"))
        setup_dve = ctx.enter_context(nc.semaphore("setup_dve"))

        def count(sem, g, k, back=0):
            n = g * PER[sem] + (k - back * PER[sem])
            return (zero_ready, 4) if isinstance(n, int) and n <= 0 else (SEM[sem], n)

        def apart(eng, g):
            if not isinstance(g, int):
                eng.sem_inc(parted, 1)

        def unit(k):
            return prob[:, k - k % 2:k - k % 2 + 2, :, k % 2, :]

        def rows_of(ap):
            return ap.rearrange("p t h n -> p (t h) n")

        def bank_of(fill, i):
            return bank[BANK[(fill, i)][0]]

        def filled(fill, i, g, back=0):
            b, c = BANK[(fill, i)]
            n = g * PER_BANK[b] + (c + 1 - back * PER_BANK[b])
            return (zero_ready, 4) if isinstance(n, int) and n <= 0 else (full[b], n)

        def emptied(fill, i, g):
            b, (f, j), back = BEFORE[(fill, i)]
            if f in ("s_even", "s_odd"):
                return count("shift_ready", g, 2 * j + 1 + (f == "s_odd"), back)
            return count(READ_OUT[f], g, j + 1, back)

        def now_full(ins, fill, i):
            ins.then_inc(full[BANK[(fill, i)][0]], 1)

        def rounds(eng, body):
            body(0, None, None, None)
            body(1, 0, None, None)
            body(2, 1, 0, None)
            with eng.Fori(1, GRP - 2) as g:
                body(g + 2, g + 1, g, g - 1)
            body(None, GRP - 1, GRP - 2, GRP - 3)
            body(None, None, GRP - 1, GRP - 2)
            body(None, None, None, GRP - 1)

        def run(steps, n, a, b, c):
            group = {"N": n, "A": a, "B": b, "C": c}
            for stream, name, i in SCHEDULE:
                if group[stream] is not None and name in steps:
                    steps[name](group[stream], i)

        x_g = x.rearrange("(g t h) n d -> g (h n) t d", t=T, h=2)
        out_g = out.rearrange("(g t h) n d -> g (h n) t d", t=T, h=2)
        xT_g = x_t.rearrange("(c p) (g n) -> g p c n", p=P, n=TOK)
        adj_g = adj.rearrange("(g t h) n m -> g (h n) t m", t=T, h=2)
        adj_h = adj.rearrange("(g t h) n m -> g h n t m", t=T, h=2)
        mask_g = mask_rows.rearrange("a (g n) -> g a n", n=T * (P + N))

        block = ctx.enter_context(nc.Block())

        @block.sync
        def _(sp):
            sp.dma_start(mcst[:, :], mrow_c).then_inc(early_in, 16)
            sp.dma_start(ident[:, :], ident_c).then_inc(early_in, 16)
            sp.dma_start(onesf, ones3_c).then_inc(early_in, 16)

            def load(n, a, b):
                if n is not None:
                    sp.wait_ge(*count("xT_lo", n, 2, 1))
                    for c in range(C):
                        sp.dma_start(xTin[:, c, :], xT_g[n][:, c, :]).then_inc(SEM["xT_in"], 16)
                if a is not None:
                    sp.wait_ge(*count("mask_rows", a, 2, 1))
                    apart(sp, a)
                    sp.dma_start(masks[:, :], mask_g[a]).then_inc(SEM["mask_in"], 16)
                    sp.wait_ge(*count("mix_sum", a, 1, 1))
                    sp.dma_start(adjA[:, :, :], adj_g[a]).then_inc(SEM["adjA_in"], 16)
                    sp.wait_ge(*count("sum0_ready", a, 2, 1))
                    sp.dma_start(xin[:, :, :], x_g[a]).then_inc(SEM["x_in"], 16)
                if b is not None:
                    sp.wait_ge(*count("meanA_ready", b, 1, 1))
                    sp.wait_ge(*count("sim_ready", b, 1, 1))
                    if isinstance(b, int) and b == 0:
                        sp.wait_ge(zero_ready, 1)
                    for h in range(2):
                        sp.dma_start(adjB[h * N:(h + 1) * N, :, h * N:(h + 1) * N],
                                     adj_h[b, h]).then_inc(SEM["adjB_in"], 16)

            def store(b):
                for i in range(2):
                    sp.wait_ge(*count("x4_ready", b, i + 1))
                    sp.dma_start(out_g[b][:, 2 * i:2 * i + 2, :],
                                 xl[3][:, 2 * i:2 * i + 2, :]).then_inc(SEM["out_done"], 16)

            load(0, None, None)
            def matrix(dst, src):
                sp.dma_start(dst, src.rearrange("(c k) n -> k c n", k=P)).then_inc(weights_in, 16)

            for i, w in enumerate((raw_q, raw_k, raw_v)):
                sp.dma_start(w, wqkv[i].rearrange("(c k) n -> k c n", k=P)).then_inc(qkv_in[i], 16)
            sp.dma_start(raw_o, w_out.rearrange("(c k) n -> k c n", k=P)).then_inc(wo_in, 16)
            load(1, 0, None)
            matrix(raw_1, w1_t)
            sp.wait_ge(weights_ready, 1)
            matrix(raw_2, w2_t)
            matrix(raw_m, w_mean_t)
            matrix(raw_qk, wqk_t)
            sp.wait_ge(weights_ready, 2)
            matrix(raw_lr[:, 0:C, :], wl_t)
            matrix(raw_lr[:, C:2 * C, :], wr_t)
            sp.dma_start(bqk[:, :], bqk_c).then_inc(weights_in, 16)
            sp.dma_start(row0, adj_row0).then_inc(weights_in, 16)
            load(2, 1, 0)
            with sp.Fori(1, GRP - 2) as g:
                load(g + 2, g + 1, g)
                store(g - 1)
            load(None, GRP - 1, GRP - 2)
            store(GRP - 3)
            load(None, None, GRP - 1)
            store(GRP - 2)
            store(GRP - 1)
            sp.wait_ge(*count("out_done", GRP - 1, 32))

        @block.gpsimd
        def _(pool):
            pool.memset(adjB[:, :, :], 0.0).then_inc(zero_ready, 1)
            pool.memset(negh[:, :], -0.5).then_inc(zero_ready, 1)
            pool.memset(bias3[:, :], 0.0).then_inc(zero_ready, 1)
            pool.memset(onescol[:, :], 1.0).then_inc(zero_ready, 1)
            pool.wait_ge(zero_ready, 4)

            def residual(g, i):
                if isinstance(g, int) and g == 0:
                    pool.wait_ge(bias_in, 16 * 8)
                pool.wait_ge(*count("x_in", g, 16))
                pool.tensor_tensor(xin[:, :, :], xin[:, :, :],
                                   bout[:, :].rearrange("p (a d) -> p a d", a=1).broadcast_to([P, T, D]),
                                   ALU.add).then_inc(SEM["residual_ready"], 1)

            def inv_root(g, layer, name, lo, hi, k):
                pool.wait_ge(*count(f"mv{name}", g, hi))
                n = "_h" if layer == 4 else str(layer)
                apart(pool, g)
                pool.tensor_scalar(var[layer][:, lo:hi], mv[layer][:, lo:hi, 1], EPS_LN, None,
                                   ALU.add).then_inc(SEM[f"var{n}"], 1)
                pool.wait_ge(*count(f"var{n}", g, k + 1))
                pool.tensor_tensor(rstd[layer][:, lo:hi], var[layer][:, lo:hi], negh[:, lo:hi],
                                   ALU.pow).then_inc(SEM[f"rstd{n}"], 1)

            def graph_a(g, i):
                pool.wait_ge(*count("rdeg_ready", g, 1))
                pool.wait_ge(*count("adjB_in", g, 32))
                pool.wait_ge(*filled("meanT", 0, g, 1))
                pool.tensor_tensor(meanA[:, :, :], adjB[:, :, :],
                                   rdeg[:, :].rearrange("p (t a) -> p t a", a=1).broadcast_to([P, T, P]),
                                   ALU.mult).then_inc(SEM["meanA_ready"], 1)

            def graph_b(g, i):
                pool.wait_ge(*count("be_ready", g, 1))
                pool.wait_ge(*count("ht_ready", g, 1))
                pool.tensor_tensor(bhT[:, :, :], hT0[:, :, :],
                                   be[:, :].rearrange("p (t a) -> p t a", a=1).broadcast_to([P, T, P]),
                                   ALU.mult).then_inc(SEM["bht_ready"], 1)

            def gate_argument(g, i):
                pool.wait_ge(*filled("turn_h", HC - 1, g))
                pool.tensor_tensor(gate[:, :, :], wd[:, :].rearrange("p (a d) -> p a d", a=1).broadcast_to([P, T, D]),
                                   deg[:, :].rearrange("p (t a) -> p t a", a=1).broadcast_to([P, T, D]),
                                   ALU.mult).then_inc(SEM["z_ready"], 1)
                pool.wait_ge(*count("z_ready", g, 1))
                pool.tensor_tensor(gate[:, :, :], gate[:, :, :],
                                   bd[:, :].rearrange("p (a d) -> p a d", a=1).broadcast_to([P, T, D]),
                                   ALU.add).then_inc(SEM["z_ready"], 1)

            def split_low(g, i):
                for c in range(C):
                    pool.wait_ge(*count("xT_hi", g, c + 1))
                    pool.tensor_tensor(xT[1][:, c, :], xTin[:, c, :], xT[0][:, c, :].bitcast(F32),
                                       ALU.subtract).then_inc(SEM["xT_lo"], 1)

            def soft(g, k):
                u = unit(k)
                pool.wait_ge(*count("rsum_ready", g, k + 1))
                pool.tensor_tensor(rows_of(u), rows_of(u), srec[:, k, :].rearrange("p (h a) -> p h a", a=1)
                                   .broadcast_to([P, 2 * HP, N]), ALU.mult).then_inc(SEM["prob_ready"], 1)
                pool.wait_ge(*count("prob_ready", g, k + 1))
                pool.wait_ge(*count("mix_ready", g, 1))
                t = k - k % 2
                pool.tensor_tensor(u, u, mix[:, t:t + 2, :].rearrange("p t (a n) -> p t a n", a=1)
                                   .broadcast_to([P, 2, HP, N]), ALU.add).then_inc(SEM["attn_ready"], 1)

            steps = {
                "soft": soft, "mask": residual,
                "norm0": lambda g, i: inv_root(g, 0, "0", 2 * i, 2 * i + 2, i),
                "graph_a": graph_a, "graph_b": graph_b, "gate": gate_argument, "split_low": split_low,
                "mean": lambda g, i: inv_root(g, 1, "1", 2 * i, 2 * i + 2, i),
                "hyper": lambda g, i: inv_root(g, 2, "2", 2 * i, 2 * i + 2, i),
                "out3": lambda g, i: inv_root(g, 3, "3", 2 * i, 2 * i + 2, i),
                "up": lambda g, i: inv_root(g, 4, "_h", i, i + 1, i),
            }
            rounds(pool, lambda n, a, b, c: run(steps, n, a, b, c))

        @block.scalar
        def _(act):
            def row(ap, n=P):
                return ap.rearrange("(a n) -> a n", a=1).broadcast_to([n, ap.shape[0]])

            act.dma_start(gam[:, :], gamma_c).then_inc(bias_in, 16)
            act.dma_start(bet[:, :], beta_c).then_inc(bias_in, 16)
            act.dma_start(b1row, row(b1, 1)).then_inc(bias_in, 16)
            act.dma_start(b2row[:, 0:D], row(b2, 1)).then_inc(bias_in, 16)
            act.dma_start(b2row[:, D:2 * D], row(bl, 1)).then_inc(bias_in, 16)
            act.dma_start(bout[:, :], row(b_out)).then_inc(bias_in, 16)
            act.dma_start(wd[:, :], row(wd_r)).then_inc(bias_in, 16)
            act.dma_start(bd[:, :], row(bd_r)).then_inc(bias_in, 16)

            act.wait_ge(zero_ready, 4)
            act.activation(warm[:, :], negh[:, :], ACT.Exp)

            def split(g, i):
                for c in range(C):
                    act.wait_ge(*count("xT_in", g, 32))
                    act.wait_ge(*filled("v", T - 1, g, 1))
                    act.activation(xT[0][:, c, :], xTin[:, c, :], ACT.Copy).then_inc(SEM["xT_hi"], 1)

            def copy_out(g, fill, i, dst, ready, func=ACT.Copy, **kw):
                act.wait_ge(*filled(fill, i, g))
                src = bank_of(fill, i)
                act.activation(dst, src[:, :], func, **kw).then_inc(SEM[ready], 1)

            def mixmat(g, i):
                act.wait_ge(*count("adjA_in", g, 16))
                act.activation(expA[:, :, :], adjA[:, :, :], ACT.Exp, scale=-1.0).then_inc(SEM["expA_ready"], 1)

            def val(g, i):
                act.wait_ge(*filled("v", i, g))
                src = bank_of("v", i)[:, :].rearrange("n (p e d) -> n e p d", e=2, d=DH)
                for gr in range(2):
                    for e in range(2):
                        ins = act.activation(v[e * N:(e + 1) * N, i, gr, :, :], src[gr * N:(gr + 1) * N, e], ACT.Copy)
                ins.then_inc(SEM["v_ready"], 1)

            def shift(g, k):
                act.wait_ge(*count("shift_ready", g, k + 1))
                act.activation(rows_of(unit(k)), rows_of(unit(k)), ACT.Exp,
                               scale=float(DH) ** -0.5).then_inc(SEM["exp_ready"], 1)

            def pv(g, i):
                act.wait_ge(*filled("oT", i, g))
                src = bank_of("oT", i)
                ins = act.activation(oT[0][:, :, (i % 2) * P:(i % 2 + 1) * P],
                                     src[:, :].rearrange("p (a n) -> p a n", a=HP), ACT.Copy)
                ins.then_inc(SEM["oT_hi"], 1)

            def graph_a(g, i):
                act.wait_ge(*filled("ht", 0, g))
                src = bank_of("ht", 0)
                act.activation(flat(hTb[:, :, :]), src[:, 0:T * P // 2].bitcast(BF16), ACT.Copy)
                ins = act.activation(flat(hT0[:, :, :]), src[:, 0:T * P // 2].bitcast(BF16), ACT.Copy)
                ins.then_inc(SEM["ht_ready"], 1)

            def up(g, i):
                copy_out(g, "up", i, r[:, i, :], "relu_ready", ACT.Relu)

            def down(g, i):
                copy_out(g, "down", i, flat(yw[:, 2 * i:2 * i + 2, :]), "down_ready")

            def hyper(g, i):
                act.wait_ge(*count("z_ready", g, 2))
                act.activation(gate[:, 2 * i:2 * i + 2, :], gate[:, 2 * i:2 * i + 2, :], ACT.Tanh,
                               scale=0.5).then_inc(SEM["gate_ready"], 1)

            def qk(g, i):
                copy_out(g, "qk", i, qkT[:, i, :], "qk_tanh", ACT.Tanh, scale=0.25, bias=bqk[:, i:i + 1])

            steps = {
                "split": split, "mixmat": mixmat, "v": val, "shift": shift, "pv": pv, "graph_a": graph_a, "up": up,
                "down": down, "hyper": hyper, "qk": qk,
                "q": lambda g, i: copy_out(g, "q", i, qT[:, i, :], "q_ready"),
                "k": lambda g, i: copy_out(g, "k", i, kT[:, i, :], "k_ready"),
                "turnp": lambda g, i: copy_out(g, "pT", i, pT[:, i % 2].rearrange("p a n -> p (a n)"), "pT_ready"),
                "turn1": lambda g, i: copy_out(g, "turn1", i, x1T[0][:, i, :], "turn1_hi"),
                "agg": lambda g, i: copy_out(g, "agg", i, aggT[0][:, i, :], "agg_hi"),
                "graph_m": lambda g, i: copy_out(g, "meanT", 0, flat(meanT[:, :, :]), "meanT_ready"),
                "graph_d": lambda g, i: copy_out(g, "gT", 0, flat(gT[:, :, :]), "gT_ready"),
                "spread": lambda g, i: copy_out(g, "spread", i, spT[0][:, i, :], "spread_hi"),
                "turn_h": lambda g, i: copy_out(g, "turn_h", i, hT[0][:, i, :], "hT_hi"),
                "turn3": lambda g, i: copy_out(g, "turn3", i, xgT[0][:, i, :], "turn3_hi"),
                "turn_s": lambda g, i: copy_out(g, "turn_s", 0, flat(sT[:, :, :]), "sT_ready"),
                "agg3": lambda g, i: copy_out(g, "agg3", i, agg3[0][:, i, :], "agg3_hi"),
            }
            rounds(act, lambda n, a, b, c: run(steps, n, a, b, c))

        @block.vector
        def _(dve):
            done = [0]

            def setup(ins):
                done[0] += 1
                ins.then_inc(setup_dve, 1)
                dve.wait_ge(setup_dve, done[0])

            dve.wait_ge(early_in, 16 * 3)
            dve.tensor_copy(identb[:, :], ident[:, :]).then_inc(setup_dve, 1)
            dve.tensor_copy(ones3[:, :], onesf).then_inc(setup_dve, 1)
            done[0] = 2

            def split_weight(pair, src):
                setup(dve.tensor_copy(pair[0][:, :, :], src))
                dve.tensor_tensor(pair[1][:, :, :], src, pair[0][:, :, :].bitcast(F32),
                                  ALU.subtract).then_inc(weights_ready, 1)

            for k, (pair, src) in enumerate(((wq, raw_q), (wk, raw_k), (wv, raw_v))):
                dve.wait_ge(qkv_in[k], 16)
                split_weight(pair, src)
            dve.wait_ge(wo_in, 16)
            setup(dve.tensor_scalar(raw_o, raw_o, MIX, None, ALU.mult))
            split_weight(wo, raw_o)

            def wide(ap, n):
                return ap.rearrange("p (t a) -> p t a", a=1).broadcast_to([ap.shape[0], ap.shape[1], n])

            def low_part(g, fill, i, lo, hi, name):
                dve.wait_ge(*count(f"{name}_hi", g, i + 1))
                src = bank_of(fill, i)[:, :]
                if len(lo.shape) == 3:
                    src = src.rearrange("p (a n) -> p a n", a=lo.shape[1])
                dve.tensor_tensor(lo, src, hi.bitcast(F32), ALU.subtract).then_inc(SEM[f"{name}_lo"], 1)

            def low_chunk(pair, fill, name):
                return lambda g, i: low_part(g, fill, i, pair[1][:, i, :], pair[0][:, i, :], name)

            def three_parts(dst, src, first, second):
                setup(dve.tensor_copy(dst[0], src))
                setup(dve.tensor_tensor(first, src, dst[0], ALU.subtract))
                setup(dve.tensor_copy(dst[1], first))
                setup(dve.tensor_copy(second, dst[1]))
                setup(dve.tensor_tensor(second, first, second, ALU.subtract))
                setup(dve.tensor_copy(dst[2], second))

            def bias_parts(src, lo, n):
                three_parts([bias3[row:row + 1, lo:lo + n] for row in (0, 32, 64)], src,
                            scratch_rows[0][:, 0:n], scratch_rows[1][:, 0:n])

            def other_weights(i):
                if i == 0:
                    dve.wait_ge(weights_in, 16 * 8)
                    split_weight(w1, raw_1)
                    dve.wait_ge(bias_in, 16 * 8)
                    dve.wait_ge(zero_ready, 4)
                    bias_parts(b2row, HID, 2 * D)
                if i == 1:
                    bias_parts(b1row, 0, HID)
                    split_weight(wm, raw_m)
                    split_weight(wqk, raw_qk)
                if i == 2:
                    three_parts([row0p[:, :, k] for k in range(3)], row0, gmat[:, 0, 0:T * GRP],
                                gT[:, 0, 0:T * GRP])
                    dve.wait_ge(t_full, 1)
                    setup(dve.tensor_copy(trow, bank[7][0:1, 0:D]))
                    bias_parts(trow, HID + 2 * D, D)
                if i == 3:
                    setup(dve.tensor_scalar(raw_lr, raw_lr, 0.5, None, ALU.mult))
                    setup(dve.tensor_scalar(bqk[:, :], bqk[:, :], 0.5, None, ALU.mult))
                    split_weight(wlr, raw_lr)
                if i == 4:
                    for c in range(HC):
                        ins = dve.tensor_scalar(raw_2[:, c, :], raw_2[:, c, :], gam[:, c:c + 1], None, ALU.mult)
                    setup(ins)
                    split_weight(w2, raw_2)

            def pv(g, i):
                at = slice((i % 2) * P, (i % 2 + 1) * P)
                low_part(g, "oT", i, oT[1][:, :, at], oT[0][:, :, at], "oT")
                if isinstance(g, int) and g == 0 and i < 2:
                    other_weights(i)

            def moments(g, layer, src, lo, hi):
                n = "_h" if layer == 4 else str(layer)
                for t in range(lo, hi):
                    dve.bn_stats(stats[layer][:, t, :], src[:, t, :]).then_inc(SEM[f"stats{n}"], 1)
                for t in range(lo, hi):
                    dve.wait_ge(*count(f"stats{n}", g, t + 1))
                    apart(dve, g)
                    dve.bn_aggr(mv[layer][:, t, :], stats[layer][:, t, :]).then_inc(SEM[f"mv{n}"], 1)

            def scale(g, layer, x, lo, hi, ready, k):
                n = "_h" if layer == 4 else str(layer)
                dve.wait_ge(*count(f"rstd{n}", g, k + 1))
                for t in range(lo, hi):
                    ins = dve.tensor_scalar(x[:, t, :], x[:, t, :], mv[layer][:, t, 0:1],
                                            rstd[layer][:, t:t + 1], ALU.subtract, ALU.mult)
                ins.then_inc(SEM[ready], 1)

            def mask(g, i):
                dve.wait_ge(*count("mask_in", g, 16))
                dve.scalar_tensor_tensor(out=mi[:, :, :], in0=masks[:, 0:T * P].rearrange("p (t n) -> p t n", n=P),
                                         scalar=mcst[:, 0:1], in1=mcst[:, 1:1 + P].rearrange("p (a n) -> p a n", a=1)
                                         .broadcast_to([4, T, P]), op0=ALU.max, op1=ALU.mult)\
                   .then_inc(SEM["mask_rows"], 1)
                dve.tensor_scalar(flat(mj[:, :, :]), masks[:, T * P:T * (P + N)], mcst[:, 0:1], None,
                                  ALU.max).then_inc(SEM["mask_rows"], 1)

            def mixmat(g, i):
                dve.wait_ge(*filled("mixmat", 0, g))
                src = bank_of("mixmat", 0)
                ins = dve.tensor_scalar(flat(mm01[:, :, :]), src[:, 0:T * N], 1.0 / BIG, 1.0, ALU.mult, ALU.add)
                ins.then_inc(SEM["mm_ready"], 1)
                dve.wait_ge(*count("expA_ready", g, 1))
                dve.wait_ge(*count("adjA_in", g, 16))
                dve.tensor_tensor(mix[:, :, :], expA[:, :, :], adjA[:, :, :], ALU.add).then_inc(SEM["mix_sum"], 1)
                dve.wait_ge(*count("mm_ready", g, 1))
                dve.wait_ge(*count("mix_sum", g, 1))
                dve.tensor_tensor(mix[:, :, :], mix[:, :, :], mm01[:, :, :], ALU.mult).then_inc(SEM["mix_ready"], 1)

            def shift(g, k):
                fill = "s_odd" if k % 2 else "s_even"
                dve.wait_ge(*filled(fill, k // 2, g))
                src = bank_of(fill, k // 2)[:, :].rearrange("p (h n) -> p h n", n=N)
                dve.tensor_reduce(smax[:, k, :], src, AX.X, ALU.max).then_inc(SEM["max_ready"], 1)
                dve.wait_ge(*count("max_ready", g, k + 1))
                dve.tensor_tensor(rows_of(unit(k)), src, wide(smax[:, k, :], N),
                                  ALU.subtract).then_inc(SEM["shift_ready"], 1)

            def soft(g, k):
                dve.wait_ge(*count("exp_ready", g, k + 1))
                dve.tensor_reduce(ssum[:, k, :], rows_of(unit(k)), AX.X, ALU.add).then_inc(SEM["sum_ready"], 1)
                dve.wait_ge(*count("sum_ready", g, k + 1))
                dve.reciprocal(srec[:, k, :], ssum[:, k, :]).then_inc(SEM["rsum_ready"], 1)

            def norm0(g, i):
                lo, hi = 2 * i, 2 * i + 2
                dve.wait_ge(*filled("out0", i, g))
                src = bank_of("out0", i)
                dve.wait_ge(*count("residual_ready", g, 1))
                ins = dve.tensor_tensor(flat(xl[0][:, lo:hi, :]), src[:, :], flat(xin[:, lo:hi, :]), ALU.add)
                ins.then_inc(SEM["sum0_ready"], 1)
                dve.wait_ge(*count("sum0_ready", g, i + 1))
                moments(g, 0, xl[0], lo, hi)
                if isinstance(g, int) and g == 0 and i == 0:
                    other_weights(2)

            def scale0(g, i):
                scale(g, 0, xl[0], 2 * i, 2 * i + 2, "x1_ready", i)
                if isinstance(g, int) and g == 0 and i == 1:
                    other_weights(3)

            def graph_a(g, i):
                dve.wait_ge(*count("adjB_in", g, 32))
                dve.tensor_scalar(edge[:, :, :], adjB[:, :, :], 0.0, None, ALU.not_equal).then_inc(SEM["edge_ready"], 1)
                dve.tensor_reduce(deg[:, :], adjB[:, :, :], AX.X, ALU.add).then_inc(SEM["deg_ready"], 1)
                dve.wait_ge(*count("deg_ready", g, 1))
                dve.tensor_scalar(degm[:, :], deg[:, :], 1e-6, None, ALU.max).then_inc(SEM["degmax"], 1)
                dve.wait_ge(*count("degmax", g, 1))
                dve.reciprocal(rdeg[:, :], degm[:, :]).then_inc(SEM["rdeg_ready"], 1)

            def graph_b(g, i):
                dve.wait_ge(*filled("cnt", 0, g))
                src = bank_of("cnt", 0)
                dve.tensor_scalar(cntm[:, :], src[:, 0:T], 1.0, None, ALU.max).then_inc(SEM["cntmax"], 1)
                dve.tensor_reduce(dsum[:, :], src[:, T:4 * T].rearrange("p (t k) -> p t k", k=3), AX.X,
                                  ALU.add).then_inc(SEM["dsum"], 1)
                dve.wait_ge(*count("cntmax", g, 1))
                dve.reciprocal(be[:, :], cntm[:, :]).then_inc(SEM["be_ready"], 1)
                dve.wait_ge(*count("dsum", g, 1))
                dve.tensor_scalar(dpos[:, :], dsum[:, :], 0.0, None, ALU.is_gt).then_inc(SEM["dsign"], 1)
                dve.tensor_scalar(dneg[:, :], dsum[:, :], 0.0, None, ALU.is_le).then_inc(SEM["dsign"], 1)
                dve.wait_ge(*count("dsign", g, 2))
                ins = dve.scalar_tensor_tensor(out=dsafe[:, :], in0=dsum[:, :], scalar=0.0, in1=dneg[:, :],
                                               op0=ALU.max, op1=ALU.add)
                ins.then_inc(SEM["dsafe"], 1)
                dve.wait_ge(*count("dsafe", g, 1))
                dve.reciprocal(drec[:, :], dsafe[:, :]).then_inc(SEM["drec"], 1)
                dve.wait_ge(*count("drec", g, 1))
                dve.tensor_tensor(dn[:, :], drec[:, :], dpos[:, :], ALU.mult).then_inc(SEM["dn_ready"], 1)

            def graph_c(g, i):
                dve.wait_ge(*filled("sym", 0, g))
                src = bank_of("sym", 0)
                dve.wait_ge(*count("dn_ready", g, 1))
                ins = dve.tensor_tensor(gmat[:, :, :], src[:, :].rearrange("p (t n) -> p t n", t=T),
                                        wide(dn[:, :], P), ALU.mult)
                ins.then_inc(SEM["g_ready"], 1)

            def mean(g, i):
                if isinstance(g, int) and g == 0 and i == 0:
                    other_weights(4)
                lo, hi = 2 * i, 2 * i + 2
                dve.wait_ge(*filled("mean", i, g))
                src = bank_of("mean", i)
                dve.wait_ge(*count("x1_ready", g, 2))
                dve.wait_ge(*count("out_done", g, 32, 1))
                ins = dve.scalar_tensor_tensor(out=flat(xl[1][:, lo:hi, :]), in0=src[:, :], scalar=0.0,
                                               in1=flat(xl[0][:, lo:hi, :]), op0=ALU.max, op1=ALU.add)
                ins.then_inc(SEM["sum1_ready"], 1)
                dve.wait_ge(*count("sum1_ready", g, i + 1))
                moments(g, 1, xl[1], lo, hi)

            def up(g, i):
                dve.wait_ge(*count("relu_ready", g, i + 1))
                moments(g, 4, r, i, i + 1)
                if i > 0:
                    scale(g, 4, r, i - 1, i, "h_ready", i - 1)
                if i == T - 1:
                    scale(g, 4, r, i, i + 1, "h_ready", i)

            def qk(g, i):
                dve.wait_ge(*count("qk_tanh", g, i + 1))
                dve.tensor_scalar(qkT[:, i, :], qkT[:, i, :], 1.0, None, ALU.add).then_inc(SEM["qk_ready"], 1)

            def hyper(g, i):
                lo, hi = 2 * i, 2 * i + 2
                dve.wait_ge(*filled("hyper", i, g))
                src = bank_of("hyper", i)
                dve.wait_ge(*count("x2_ready", g, 2))
                ins = dve.scalar_tensor_tensor(out=flat(xl[2][:, lo:hi, :]), in0=flat(xl[1][:, lo:hi, :]), scalar=2.0,
                                               in1=src[:, :], op0=ALU.mult, op1=ALU.add)
                ins.then_inc(SEM["sum2_ready"], 1)
                dve.wait_ge(*count("sum2_ready", g, i + 1))
                moments(g, 2, xl[2], lo, hi)

            def gated(g, k):
                scale(g, 2, xl[2], 2 * k, 2 * k + 2, "x3_ready", k)
                dve.wait_ge(*count("x3_ready", g, k + 1))
                dve.wait_ge(*count("gate_ready", g, k + 1))
                dve.scalar_tensor_tensor(out=flat(xg[:, 2 * k:2 * k + 2, :]),
                                         in0=flat(gate[:, 2 * k:2 * k + 2, :]), scalar=1.0,
                                         in1=flat(xl[2][:, 2 * k:2 * k + 2, :]),
                                         op0=ALU.add, op1=ALU.mult).then_inc(SEM["xg_ready"], 1)

            def simi(g, i):
                dve.wait_ge(*filled("sim", 0, g))
                src = bank_of("sim", 0)
                dve.wait_ge(*count("adjB_in", g, 32))
                ins = dve.tensor_tensor(flat(sim[:, :, :]), src[:, :], flat(adjB[:, :, :]), ALU.mult)
                ins.then_inc(SEM["sim_ready"], 1)
                dve.wait_ge(*count("sim_ready", g, 1))
                dve.tensor_reduce(simsum[:, :], sim[:, :, :], AX.X, ALU.add).then_inc(SEM["simsum"], 1)
                dve.wait_ge(*count("simsum", g, 1))
                dve.tensor_scalar(simeps[:, :], simsum[:, :], 64e-6, None, ALU.add).then_inc(SEM["simeps"], 1)
                dve.wait_ge(*count("simeps", g, 1))
                dve.reciprocal(simrec[:, :], simeps[:, :]).then_inc(SEM["simrec"], 1)
                dve.wait_ge(*count("simrec", g, 1))
                dve.tensor_tensor(smat[:, :, :], sim[:, :, :], wide(simrec[:, :], P),
                                  ALU.mult).then_inc(SEM["s_ready"], 1)

            def out3(g, i):
                lo, hi = 2 * i, 2 * i + 2
                dve.wait_ge(*filled("out3", i, g))
                src = bank_of("out3", i)
                ins = dve.scalar_tensor_tensor(out=flat(xl[3][:, lo:hi, :]), in0=src[:, :], scalar=0.0,
                                               in1=flat(xl[2][:, lo:hi, :]), op0=ALU.max, op1=ALU.add)
                ins.then_inc(SEM["sum3_ready"], 1)
                dve.wait_ge(*count("sum3_ready", g, i + 1))
                moments(g, 3, xl[3], lo, hi)

            steps = {
                "mask": mask, "mixmat": mixmat, "shift": shift, "soft": soft, "pv": pv, "norm0": norm0,
                "graph_a": graph_a, "graph_b": graph_b, "graph_c": graph_c, "mean": mean, "up": up, "hyper": hyper,
                "qk": qk, "sim": simi, "out3": out3, "gated": gated,
                "scale0": scale0,
                "scale1": lambda g, i: [scale(g, 1, xl[1], 2 * k, 2 * k + 2, "x2_ready", k) for k in range(2)],
                "scale3": lambda g, i: [scale(g, 3, xl[3], 2 * k, 2 * k + 2, "x4_ready", k) for k in range(2)],
                "turn1": low_chunk(x1T, "turn1", "turn1"), "agg": low_chunk(aggT, "agg", "agg"),
                "spread": low_chunk(spT, "spread", "spread"), "turn_h": low_chunk(hT, "turn_h", "hT"),
                "turn3": low_chunk(xgT, "turn3", "turn3"), "agg3": low_chunk(agg3, "agg3", "agg3"),
            }
            rounds(dve, lambda n, a, b, c: run(steps, n, a, b, c))

        @block.tensor
        def _(pe):
            pe.wait_ge(setup_dve, 2)

            def product(out_ap, pairs, bias=None, ready=()):
                if bias is not None:
                    pe.matmul(out_ap, ones3[0:96, :], bias3[:, bias[0]:bias[1]], start=True, stop=False)
                for j, (l, rr) in enumerate(pairs):
                    if j >= len(pairs) - len(ready):
                        pe.wait_ge(*ready[j - len(pairs) + len(ready)])
                    pe.matmul(out_ap, l[0], rr[0], start=(bias is None and j == 0), stop=False)
                    pe.matmul(out_ap, l[0], rr[1], start=False, stop=False)
                    ins = pe.matmul(out_ap, l[1], rr[0], start=False, stop=(j == len(pairs) - 1))
                return ins

            def tile_of(pair, c, t):
                return [x[:, c, t * P:(t + 1) * P] for x in pair]

            def chunk(pair, c, cols=slice(None)):
                return [x[:, c, cols] for x in pair]

            def mixmat(g, i):
                pe.wait_ge(*count("mask_rows", g, 2))
                pe.wait_ge(*emptied("mixmat", 0, g))
                dst = bank_of("mixmat", 0)
                apart(pe, g)
                for t in range(T):
                    ins = pe.matmul(dst[:, t * N:(t + 1) * N], mi[:, t, :], mj[:, t, :],
                                    start=True, stop=True)
                now_full(ins, "mixmat", 0)

            def beta_row():
                pe.wait_ge(weights_in, 16 * 8)
                pe.wait_ge(bias_in, 16 * 8)
                for c in range(HC):
                    ins = pe.matmul(bank[7][0:1, 0:D], bet[:, c:c + 1], raw_2[:, c, :], start=(c == 0),
                                    stop=(c == HC - 1))
                ins.then_inc(t_full, 1)

            def proj(name, w, g, i):
                if isinstance(g, int) and g == 0 and i == 0:
                    pe.wait_ge(weights_ready, 1 if name == "q" else 2)
                pe.wait_ge(*count("xT_lo", g, 2))
                pe.wait_ge(*emptied(name, i, g))
                dst = bank_of(name, i)
                now_full(product(dst[:, :], [(chunk(w, c, slice(i * P, (i + 1) * P)), chunk(xT, c))
                                             for c in range(C)]), name, i)

            def val(g, i):
                if isinstance(g, int) and g == 0 and i == 0:
                    pe.wait_ge(weights_ready, 3)
                pe.wait_ge(*emptied("v", i, g))
                dst = bank_of("v", i)
                now_full(product(dst[:, :], [(tile_of(xT, c, i), chunk(wv, c)) for c in range(C)]), "v", i)

            def score(g, i):
                pe.wait_ge(*count("q_ready", g, HP))
                pe.wait_ge(*count("k_ready", g, HP))
                pe.wait_ge(*emptied("s_odd", i, g))
                dst = [bank_of("s_even", i), bank_of("s_odd", i)]
                apart(pe, g)
                for e in range(2):
                    for k in range(2):
                        pe.matmul(dst[e][:, k * HP * N:(k + 1) * HP * N], mi[:, 2 * i + k, :],
                                  mj[:, 2 * i + k:2 * i + k + 1, :].broadcast_to([4, HP, N]),
                                  start=(k == 0), stop=False, skip_group_check=True)
                ins = None
                for k in range(2):
                    for p in range(HP):
                        for gr in range(2):
                            for e in range(2):
                                tok = slice((2 * i + k) * P + gr * N, (2 * i + k) * P + (gr + 1) * N)
                                col = (k * HP + p) * N
                                ins0, ins = ins, pe.matmul(dst[e][gr * N:(gr + 1) * N, col:col + N],
                                                qT[e * DH:(e + 1) * DH, p, tok], kT[e * DH:(e + 1) * DH, p, tok],
                                                start=False, stop=(k == 1 and p == HP - 1), skip_group_check=True)
                now_full(ins0, "s_even", i)
                now_full(ins, "s_odd", i)

            def turnp(g, i):
                pe.wait_ge(*count("attn_ready", g, i - i % 2 + 2))
                pe.wait_ge(*emptied("pT", i, g))
                dst = bank_of("pT", i)
                for p in range(HP):
                    ins = pe.transpose(dst[:, p * P:(p + 1) * P],
                                       prob[:, i, p].rearrange("p e n -> p (e n)"), ident[:, :])
                now_full(ins, "pT", i)

            def pv(g, i):
                pe.wait_ge(*count("pT_ready", g, i + 1))
                pe.wait_ge(*count("v_ready", g, i + 1))
                pe.wait_ge(*emptied("oT", i, g))
                dst = bank_of("oT", i)
                apart(pe, g)
                for p in range(HP):
                    for gr in range(2):
                        for e in range(2):
                            rows = slice(e * N, (e + 1) * N)
                            ins = pe.matmul(dst[rows, p * P + gr * N:p * P + (gr + 1) * N], v[rows, i, gr, p, :],
                                            pT[rows, i % 2, p, gr * N:(gr + 1) * N], start=True, stop=True,
                                            skip_group_check=True)
                now_full(ins, "oT", i)

            def two_tiles(name, i, pairs_of, bias=None, ready=()):
                dst = bank_of(name, i)
                for k in range(2):
                    ins = product(dst[:, k * D:(k + 1) * D], pairs_of(2 * i + k), bias, ready if k == 0 else ())
                now_full(ins, name, i)

            def out0(g, i):
                if isinstance(g, int) and g == 0 and i == 0:
                    beta_row()
                    pe.wait_ge(weights_ready, 4)
                pe.wait_ge(*count("oT_lo", g, 2 * i + 2))
                pe.wait_ge(*emptied("out0", i, g))
                two_tiles("out0", i, lambda t: [(tile_of(oT, p, t % 2), chunk(wo, p)) for p in range(HP)])

            def turned(name, g, i, src, ready, n):
                pe.wait_ge(*emptied(name, i, g))
                dst = bank_of(name, i)
                for t in range(T):
                    if i == 0 and t % (T // n) == 0:
                        pe.wait_ge(*count(ready, g, t * n // T + 1))
                    ins = pe.transpose(dst[:, t * P:(t + 1) * P], src[:, t, i * P:(i + 1) * P], ident[:, :])
                now_full(ins, name, i)

            def graph_a(g, i):
                pe.wait_ge(*count("edge_ready", g, 1))
                pe.wait_ge(*emptied("ht", 0, g))
                dst = bank_of("ht", 0)[:, 0:T * P // 2].bitcast(BF16)
                for t in range(T):
                    ins = pe.transpose(dst[:, t * P:(t + 1) * P], edge[:, t, :], identb[:, :])
                now_full(ins, "ht", 0)

            def graph_b(g, i):
                pe.wait_ge(*count("ht_ready", g, 1))
                pe.wait_ge(*emptied("cnt", 0, g))
                dst = bank_of("cnt", 0)
                for t in range(T):
                    pe.matmul(dst[:, t:t + 1], edge[:, t, :], onescol[:, 0:1], start=True, stop=True)
                for t in range(T):
                    ins = pe.matmul(dst[:, T + 3 * t:T + 3 * t + 3], hTb[:, t, :],
                                    row0p[:, bass.ds(g * T + t, 1), :].rearrange("p a k -> p (a k)"),
                                    start=True, stop=True)
                now_full(ins, "cnt", 0)

            def graph_c(g, i):
                pe.wait_ge(*count("bht_ready", g, 1))
                pe.wait_ge(*emptied("sym", 0, g))
                dst = bank_of("sym", 0)
                for t in range(T):
                    ins = pe.matmul(dst[:, t * P:(t + 1) * P], hT0[:, t, :], bhT[:, t, :], start=True, stop=True)
                now_full(ins, "sym", 0)

            def graph_m(g, i):
                pe.wait_ge(*count("meanA_ready", g, 1))
                pe.wait_ge(*emptied("meanT", 0, g))
                dst = bank_of("meanT", 0)
                for t in range(T):
                    ins = pe.transpose(dst[:, t * P:(t + 1) * P], meanA[:, t, :], ident[:, :])
                now_full(ins, "meanT", 0)

            def graph_d(g, i):
                pe.wait_ge(*count("g_ready", g, 1))
                pe.wait_ge(*emptied("gT", 0, g))
                dst = bank_of("gT", 0)
                for t in range(T):
                    ins = pe.transpose(dst[:, t * P:(t + 1) * P], gmat[:, t, :], ident[:, :])
                now_full(ins, "gT", 0)

            def gathered(name, g, i, src, mat, halves=None):
                pe.wait_ge(*emptied(name, i, g))
                dst = bank_of(name, i)
                for t in range(T):
                    if halves and i == 0 and t % 2 == 0:
                        pe.wait_ge(*count(halves, g, t // 2 + 1))
                    ins = pe.matmul(dst[:, t * P:(t + 1) * P], src[:, t, i * P:(i + 1) * P], mat[:, t, :],
                                    start=True, stop=True)
                now_full(ins, name, i)

            def agg(g, i):
                pe.wait_ge(*count("meanT_ready", g, 1))
                gathered("agg", g, i, xl[0], meanT)

            def mean(g, i):
                if isinstance(g, int) and g == 0 and i == 0:
                    pe.wait_ge(weights_ready, 6)
                pe.wait_ge(*count("turn1_lo", g, 2))
                pe.wait_ge(*emptied("mean", i, g))
                two_tiles("mean", i, lambda t: [(tile_of(x1T, c, t), chunk(wm, c)) for c in range(C)]
                          + [(tile_of(aggT, c, t), chunk(wm, C + c)) for c in range(C)],
                          ready=[count("agg_lo", g, c + 1) for c in range(C)])

            def spread(g, i):
                pe.wait_ge(*count("gT_ready", g, 1))
                gathered("spread", g, i, xl[1], gT, "x2_ready")

            def up(g, i):
                if isinstance(g, int) and g == 0 and i == 0:
                    pe.wait_ge(weights_ready, 9)
                pe.wait_ge(*emptied("up", i, g))
                dst = bank_of("up", i)
                now_full(product(dst[:, :], [(tile_of(spT, c, i), chunk(w1, c)) for c in range(C)], (0, HID),
                                 [count("spread_lo", g, c + 1) for c in range(C)]), "up", i)

            def down(g, i):
                pe.wait_ge(*emptied("down", i, g))
                two_tiles("down", i, lambda t: [(tile_of(hT, c, t), chunk(w2, c)) for c in range(HC)],
                          (HID + 2 * D, NBIAS), [count("hT_lo", g, c + 1) for c in range(HC)])

            def hyper(g, i):
                pe.wait_ge(*count("down_ready", g, i + 1))
                pe.wait_ge(*emptied("hyper", i, g))
                dst = bank_of("hyper", i)
                for k in range(2):
                    half = dst[:, k * D:(k + 1) * D]
                    pe.matmul(half, ones3[0:96, :], bias3[:, HID:HID + D], start=True, stop=False)
                    ins = pe.matmul(half, gT[:, 2 * i + k, :], yw[:, 2 * i + k, :], start=False, stop=True)
                now_full(ins, "hyper", i)

            def qk(g, i):
                pe.wait_ge(*emptied("qk", i, g))
                dst = bank_of("qk", i)
                now_full(product(dst[:, :], [(chunk(wqk, c, slice(i * P, (i + 1) * P)), chunk(xgT, c))
                                             for c in range(C)],
                                 ready=[count("turn3_lo", g, c + 1) for c in range(C)]), "qk", i)

            def simi(g, i):
                pe.wait_ge(*count("qk_ready", g, 2))
                pe.wait_ge(*emptied("sim", 0, g))
                dst = bank_of("sim", 0)
                for t in range(T):
                    for c in range(C):
                        tile = qkT[:, c, t * P:(t + 1) * P]
                        ins = pe.matmul(dst[:, t * P:(t + 1) * P], tile, tile, start=(c == 0), stop=(c == C - 1))
                now_full(ins, "sim", 0)

            def turn_s(g, i):
                pe.wait_ge(*count("s_ready", g, 1))
                pe.wait_ge(*emptied("turn_s", 0, g))
                dst = bank_of("turn_s", 0)
                for t in range(T):
                    ins = pe.transpose(dst[:, t * P:(t + 1) * P], smat[:, t, :], ident[:, :])
                now_full(ins, "turn_s", 0)

            def agg3_(g, i):
                pe.wait_ge(*count("sT_ready", g, 1))
                gathered("agg3", g, i, xg, sT)

            def out3(g, i):
                pe.wait_ge(*emptied("out3", i, g))
                two_tiles("out3", i, lambda t: [(tile_of(xgT, c, t), chunk(wlr, C + c)) for c in range(C)]
                          + [(tile_of(agg3, c, t), chunk(wlr, c)) for c in range(C)], (HID + D, HID + 2 * D),
                          [count("agg3_lo", g, c + 1) for c in range(C)])

            steps = {
                "mixmat": mixmat, "q": lambda g, i: proj("q", wq, g, i), "k": lambda g, i: proj("k", wk, g, i),
                "v": val, "score": score, "turnp": turnp, "pv": pv, "out0": out0,
                "turn1": lambda g, i: turned("turn1", g, i, xl[0], "x1_ready", 2),
                "graph_a": graph_a, "graph_b": graph_b, "graph_m": graph_m, "graph_c": graph_c, "graph_d": graph_d,
                "agg": agg,
                "mean": mean, "spread": spread, "up": up,
                "turn_h": lambda g, i: turned("turn_h", g, i, r, "h_ready", T),
                "down": down, "hyper": hyper,
                "turn3": lambda g, i: turned("turn3", g, i, xg, "xg_ready", 2),
                "qk": qk, "sim": simi, "turn_s": turn_s, "agg3": agg3_, "out3": out3,
            }
            rounds(pe, lambda n, a, b, c: run(steps, n, a, b, c))


def kernel(**inputs):
    import numpy as _np
    import concourse.bacc as _bacc
    from concourse import mybir as _mybir
    from concourse.bass_utils import run_bass_kernel_spmd as _run

    a = {k: _np.asarray(v) for k, v in inputs.items()}
    ident = _np.eye(P, dtype=_np.float32)
    ones3 = _np.zeros((P, P), _np.float32)
    ones3[[0, 32, 64]] = 1.0
    mrow = _np.zeros((4, 1 + P), _np.float32)
    mrow[:, 0] = [1, 0, 1, 0]
    mrow[0:2, 1:1 + N] = [[-BIG], [BIG]]
    mrow[2:4, 1 + N:] = [[-BIG], [BIG]]
    m = a["nodemask"]
    rows = _np.broadcast_to(m.reshape(1, GRP, T * P), (4, GRP, T * P))
    cols = _np.repeat(_np.moveaxis(m.reshape(GRP, T, 2, N), 2, 0), 2, axis=0).reshape(4, GRP, T * N)
    arrays = {
        "x": a["x"], "x_t": a["x"].reshape(B * N, D).T, "adj": a["adj"],
        "adj_row0": a["adj"][:, 0, :].reshape(B // 2, P).T,
        "mask_rows": _np.concatenate([rows, cols], axis=2).reshape(4, -1),
        "wqkv": _np.moveaxis(a["L0_gnn_W_qkv"].reshape(D, H, 3, DH), 2, 0).reshape(3, D, H * DH),
        "w_out": a["L0_gnn_W_out"], "b_out": a["L0_gnn_b_out"],
        "w_mean_t": a["L1_gnn_W"].T, "w1_t": a["L2_gnn_W1"].T, "b1": a["L2_gnn_b1"],
        "gamma_c": a["L2_gnn_gamma"].reshape(HC, P).T, "beta_c": a["L2_gnn_beta"].reshape(HC, P).T,
        "w2_t": a["L2_gnn_W2"].T, "b2": a["L2_gnn_b2"], "wqk_t": a["L3_gnn_Wqk"].T,
        "bqk_c": a["L3_gnn_bqk"].reshape(C, P).T, "wl_t": a["L3_gnn_Wl"].T, "bl": a["L3_gnn_bl"],
        "wr_t": a["L3_gnn_Wr"].T, "wd_r": a["L3_gnn_Wd"].reshape(D), "bd_r": a["L3_gnn_bd"],
        "ident_c": ident, "ones3_c": ones3, "mrow_c": mrow,
    }
    nc = _bacc.Bacc("TRN2", target_bir_lowering=False, num_devices=1)
    maps, args = {}, []
    for name, arr in arrays.items():
        arr = _np.ascontiguousarray(arr)
        maps[f"in_{name}"] = arr
        args.append(nc.dram_tensor(f"in_{name}", arr.shape, _mybir.dt.from_np(arr.dtype), kind="ExternalInput").ap())
    out = nc.dram_tensor("out_x", (B, N, D), F32, kind="ExternalOutput").ap()
    graph_layers(nc, *args, out)
    r = _run(nc, [maps], core_ids=[0])
    return r.results[0]["out_x"]
```
